# Optimizing a Trainium2 kernel written in Bass

```python
import numpy as np
import jax
import jax.numpy as jnp

def _softmax(x, axis=-1):
    return jax.nn.softmax(x, axis=axis)

def _gelu(x):
    return jax.nn.gelu(x, approximate=True)

def _silu(x):
    return jax.nn.silu(x)

def _sigmoid(x):
    return jax.nn.sigmoid(x)

def _layernorm(x, axis=-1, eps=1e-05):
    m = jnp.mean(x, axis=axis, keepdims=True)
    v = jnp.var(x, axis=axis, keepdims=True)
    return (x - m) / jnp.sqrt(v + eps)

def _scatter_add(tgt, idx, src, axis=0):
    return tgt.at[idx].add(src)

def _segment_sum(src, seg, n):
    return jax.ops.segment_sum(src, seg, n)
kernel_name = 'mk_adj_preln_d4_adj_r2_c8e582'

def setup_inputs(seed: int=0):
    np.random.seed(seed)
    _w = jnp.asarray

    def _rec_inputs():
        import jax
        import jax.numpy as jnp
        _gk = jax.random.key(seed)
        x = -0.001003 + 1 * jax.random.normal(jax.random.fold_in(_gk, 1), (6144, 128), jnp.float32)
        _w = (1.0 + jnp.arange(6144, dtype=jnp.float32)) ** (-0.5)
        _w = _w / _w.mean()
        _pij = jnp.clip(0.00130208 * _w[:, None] * _w[None, :], 0.0, 1.0)
        _a = jax.random.uniform(jax.random.fold_in(_gk, 2), (6144, 6144)) < _pij
        adj = _a.astype(jnp.int32)
        return (x, adj)
    x, adj = _rec_inputs()

    def _L0_gnn_setup():
        import jax, jax.numpy as jnp
        import numpy as np
        M = 6144
        N = 6144
        D = 128
        TEMPERATURE = 0.07
        NEG_PAD = jnp.float32(-2 ** 32 + 1)
        key = jax.random.key(seed)
        k1, k2, k3, k4 = jax.random.split(key, 4)
        xx_anchor = jax.random.normal(k1, (M, D), dtype=jnp.float32)
        inp = jax.random.normal(k2, (N, D), dtype=jnp.float32)
        adj = (jax.random.uniform(k3, (M, N)) < 0.002).astype(jnp.int32)
        limit = jnp.sqrt(6.0 / (D + D)).astype(jnp.float32)
        weight = jax.random.uniform(k4, (D, D), minval=-limit, maxval=limit, dtype=jnp.float32)
        return {'xx_anchor': xx_anchor, 'input': inp, 'adj': adj, 'weight': weight}
    _L0_gnn_all = _L0_gnn_setup()
    _L0_gnn_in = {k: v for k, v in _L0_gnn_all.items() if k in ('input', 'weight')}
    del _L0_gnn_all

    def _L1_gnn_setup():
        import jax, jax.numpy as jnp
        import numpy as np
        ALPHA = 0.2
        NEG_INF = -9000000000000000.0
        key = jax.random.key(seed)
        k1, k2, k3, k4 = jax.random.split(key, 4)
        N, F_IN, F_OUT = (4096, 128, 128)
        h = jax.random.normal(k1, (N, F_IN), dtype=jnp.float32)
        adj = jax.random.randint(k2, (N, N), 0, 2, dtype=jnp.int32)
        W = jax.random.normal(k3, (F_IN, F_OUT), dtype=jnp.float32) * (1.414 / np.sqrt(F_IN))
        a = jax.random.normal(k4, (2 * F_OUT, 1), dtype=jnp.float32) * (1.414 / np.sqrt(2 * F_OUT))
        return {'h': h, 'adj': adj, 'W': W, 'a': a}
    _L1_gnn_all = _L1_gnn_setup()
    _L1_gnn_in = {k: v for k, v in _L1_gnn_all.items() if k in ('W', 'a')}
    del _L1_gnn_all

    def _L2_gnn_setup():
        import jax, jax.numpy as jnp
        import numpy as np
        N = 4096
        D_IN = 128
        D_OUT = 128
        ALPHA = 0.2
        NEG = -9000000000000000.0
        key = jax.random.key(seed)
        k1, k2, k3, k4 = jax.random.split(key, 4)
        input = jax.random.normal(k1, (N, D_IN), dtype=jnp.float32)
        adj = jax.random.randint(k2, (N, N), 0, 2, dtype=jnp.int32)
        lim_w = 1.414 * np.sqrt(6.0 / (D_IN + D_OUT))
        W = jax.random.uniform(k3, (D_IN, D_OUT), jnp.float32, -lim_w, lim_w)
        lim_a = 1.414 * np.sqrt(6.0 / (2 * D_OUT + 1))
        a = jax.random.uniform(k4, (2 * D_OUT, 1), jnp.float32, -lim_a, lim_a)
        return {'input': input, 'adj': adj, 'W': W, 'a': a}
    _L2_gnn_all = _L2_gnn_setup()
    _L2_gnn_in = {k: v for k, v in _L2_gnn_all.items() if k in ('W', 'a')}
    del _L2_gnn_all

    def _L3_gnn_setup():
        import jax, jax.numpy as jnp
        import numpy as np
        ALPHA = 0.2
        NEG_BIG = -9000000000000000.0
        key = jax.random.key(seed)
        k1, k2, k3, k4 = jax.random.split(key, 4)
        N, F_IN, F_OUT = (4096, 128, 128)
        h = jax.random.normal(k1, (N, F_IN), dtype=jnp.float32)
        adj = jax.random.randint(k2, (N, N), 0, 2, dtype=jnp.int32)
        W = jax.random.normal(k3, (F_IN, F_OUT), dtype=jnp.float32) * (1.0 / np.sqrt(F_IN))
        a = jax.random.normal(k4, (2 * F_OUT, 1), dtype=jnp.float32) * (1.0 / np.sqrt(2 * F_OUT))
        return {'h': h, 'adj': adj, 'W': W, 'a': a}
    _L3_gnn_all = _L3_gnn_setup()
    _L3_gnn_in = {k: v for k, v in _L3_gnn_all.items() if k in ('W', 'a')}
    del _L3_gnn_all
    return {'x': x, 'adj': adj, 'L0_gnn_input': _L0_gnn_in['input'], 'L0_gnn_weight': _L0_gnn_in['weight'], 'L1_gnn_W': _L1_gnn_in['W'], 'L1_gnn_a': _L1_gnn_in['a'], 'L2_gnn_W': _L2_gnn_in['W'], 'L2_gnn_a': _L2_gnn_in['a'], 'L3_gnn_W': _L3_gnn_in['W'], 'L3_gnn_a': _L3_gnn_in['a']}

def reference(x, adj, L0_gnn_input, L0_gnn_weight, L1_gnn_W, L1_gnn_a, L2_gnn_W, L2_gnn_a, L3_gnn_W, L3_gnn_a):
    import jax
    import jax.numpy as jnp

    def _L0_gnn_ref(xx_anchor, input, adj, weight):
        import jax, jax.numpy as jnp
        import numpy as np
        M = 6144
        N = 6144
        D = 128
        TEMPERATURE = 0.07
        NEG_PAD = jnp.float32(-2 ** 32 + 1)
        anchor_adj = jnp.einsum('md,de,ne->mn', xx_anchor, weight, input)
        scores = jnp.where(adj > 0, anchor_adj, NEG_PAD)
        atten = jax.nn.softmax(scores / TEMPERATURE, axis=1)
        return atten @ input

    def _L1_gnn_ref(h, adj, W, a):
        import jax, jax.numpy as jnp
        import numpy as np
        ALPHA = 0.2
        NEG_INF = -9000000000000000.0
        Wh = h @ W
        F_out = W.shape[1]
        e_src = Wh @ a[:F_out, 0]
        e_dst = Wh @ a[F_out:, 0]
        e = jax.nn.leaky_relu(e_src[:, None] + e_dst[None, :], negative_slope=ALPHA)
        attention = jax.nn.softmax(jnp.where(adj > 0, e, NEG_INF), axis=1)
        h_prime = attention @ Wh
        return h_prime

    def _L2_gnn_ref(input, adj, W, a):
        import jax, jax.numpy as jnp
        import numpy as np
        N = 4096
        D_IN = 128
        D_OUT = 128
        ALPHA = 0.2
        NEG = -9000000000000000.0
        h = input @ W
        a1 = a[:D_OUT, 0]
        a2 = a[D_OUT:, 0]
        e = (h @ a1)[:, None] + (h @ a2)[None, :]
        e = jnp.where(e > 0, e, ALPHA * e)
        e = jnp.where(adj > 0, e, NEG)
        attention = jax.nn.softmax(e, axis=1)
        h_prime = attention @ h
        return jax.nn.elu(h_prime)

    def _L3_gnn_ref(h, adj, W, a):
        import jax, jax.numpy as jnp
        import numpy as np
        ALPHA = 0.2
        NEG_BIG = -9000000000000000.0
        Wh = h @ W
        F_out = Wh.shape[1]
        a1 = a[:F_out, 0]
        a2 = a[F_out:, 0]
        e = (Wh @ a1)[:, None] + (Wh @ a2)[None, :]
        e = jnp.where(e >= 0, e, ALPHA * e)
        scores = jnp.where(adj > 0, e, NEG_BIG)
        attention = jax.nn.softmax(scores, axis=1)
        return attention @ Wh
    h = jnp.maximum(_layernorm(x, axis=-1), 0.0)
    x = x + _L0_gnn_ref(h, L0_gnn_input, adj, L0_gnn_weight)
    h = jnp.maximum(_layernorm(x, axis=-1), 0.0)
    x = x + _L1_gnn_ref(h, adj, L1_gnn_W, L1_gnn_a)
    h = jnp.maximum(_layernorm(x, axis=-1), 0.0)
    x = x + _L2_gnn_ref(h, adj, L2_gnn_W, L2_gnn_a)
    h = jnp.maximum(_layernorm(x, axis=-1), 0.0)
    x = x + _L3_gnn_ref(h, adj, L3_gnn_W, L3_gnn_a)
    return x

_drawn_inputs = setup_inputs


def setup_inputs(seed=0):
    import zlib

    import numpy as np

    out = dict(_drawn_inputs(seed))
    spreads = {}
    factors = {}
    for name, (base, spread) in spreads.items():
        noise = np.random.default_rng([zlib.crc32(name.encode()), seed]).standard_normal(out[name].shape)
        drawn = base * np.exp(spread * noise) if base else spread * noise
        out[name] = jnp.asarray(drawn.astype(out[name].dtype))
    for name, factor in factors.items():
        out[name] = (out[name] * factor).astype(out[name].dtype)
    return out
```

```python
from contextlib import ExitStack

import concourse.bass as bass
from concourse import mybir

F32 = mybir.dt.float32
F32R = mybir.dt.float32r
BF16 = mybir.dt.bfloat16
I32 = mybir.dt.int32
U8 = mybir.dt.uint8
ALU = mybir.AluOpType
ACT = mybir.ActivationFunctionType
AX = mybir.AxisListType

P = 128
N = 6144
D = 128
TILES = N // P
LAYERS = 3
TEMPERATURE = 0.07
SLOPE = 0.2
EPS = 1e-5
MASKED = -2.0 ** 100

WA = 384
BLOCKS_A = N // WA
SUB_A = WA // P
PAIRS = TILES // 2
GROUP = 4
GROUPS = TILES // GROUP
SAVE = 12
SAVES = TILES // SAVE

WG = 2 * WA
BLOCKS_G = N // WG
SUB_G = WG // P
RING = 4
CREDIT = 13
E = D + 1
LN_CHUNK = 12
LN_CHUNKS = TILES // LN_CHUNK
LN_STEPS = 3 * LN_CHUNKS + 1
CONSTS = 6 + LAYERS
HEAD = 10


class Tally:

    def __init__(self, sem, base):
        self.sem, self.base, self.n = sem, base, 0

    def inc(self, instruction):
        instruction.then_inc(self.sem, 1)
        self.n += 1

    def wait(self, engine):
        engine.wait_ge(self.sem, self.base + self.n)


def ds(start, size):
    return bass.ds(start, size)


def program(nc, x_in, adj_in_d, inp_nat, inp_t, w_in, a_in, mask_scr, g_scr, out_d):
    ctx = ExitStack()
    with ctx:
        def sb(name, shape, dt):
            return ctx.enter_context(nc.sbuf_tensor(name, shape, dt))

        def sem(name):
            return ctx.enter_context(nc.semaphore(name))

        arena = sb("arena", [P, TILES * WA], F32)
        S = arena[:, :].rearrange("p (t w) -> p t w", w=WA)
        h = arena[:, 0:N].rearrange("p (t d) -> p t d", d=D)
        hT = arena[:, N:2 * N]
        third = arena[:, 2 * N:3 * N]
        sq = third.rearrange("p (t d) -> p t d", d=D)
        R = third
        zring = arena[:, 0:RING * WG].rearrange("p (s w) -> p s w", w=WG)
        pring = arena[:, RING * WG:2 * RING * WG].rearrange("p (s w) -> p s w", w=WG)
        key_hi = sb("key_hi", [P, N], F32R)
        key_lo = sb("key_lo", [P, N], F32R)
        U = sb("U", [P, TILES, E], F32)
        X = sb("X", [P, TILES, D], F32)
        adjb = sb("adjb", [P, 3, GROUP * WA], I32)
        maskb = adjb[:, :, :].rearrange("p s w -> p (s w)").bitcast(U8).rearrange(
            "p (s h k w) -> p s h k w", s=2, h=2, k=SAVE)
        notb = sb("notb", [P, 3, GROUP * WA], BF16)
        notf = notb[:, :, :].rearrange("p s w -> p (s w)").bitcast(F32)
        Wraw = notf[:, 0:4 * D].rearrange("p (l f) -> p l f", l=4)
        neg_o = notf[:, 0:WG]
        exp_o = notf[:, WG:2 * WG]
        saveb = sb("saveb", [P, 2, SAVE * WA], U8)
        savef = saveb[:, :, :].rearrange("p s w -> p (s w)").bitcast(F32)
        a_rows = savef[:, 0:LAYERS * 2 * D].rearrange("p (l f) -> p l f", l=LAYERS)
        w_dot = savef[:, LAYERS * 2 * D:LAYERS * 2 * D + D]
        G = sb("G", [P, 4 * WA], F32R)
        run_max = sb("run_max", [P, 2, WA], F32)
        o_buf = run_max[:, :, :].rearrange("p a w -> p (a w)")
        part_max = sb("part_max", [P, WA], F32)
        max_b = sb("max_b", [P, WA], F32)
        max_c = sb("max_c", [P, SUB_A], F32)
        max_rep = sb("max_rep", [P, SUB_A, P], F32)
        hsum_rep = max_rep[:, 0, :]
        identF = sb("identF", [P, P], F32)
        negI = sb("negI", [P, P], BF16)
        WX = sb("WX", [P, LAYERS, E], F32)
        Wcur = sb("Wcur", [P, E], F32)
        va1 = sb("va1", [P, LAYERS], F32)
        va1_rep = sb("va1_rep", [P, P], F32)
        sum_b = sb("sum_b", [P, D], F32)
        mean = sb("mean", [P, TILES], F32)
        var = sb("var", [P, TILES], F32)
        rstd = sb("rstd", [P, TILES], F32)
        B = sb("B", [P, TILES], F32)
        Q = sb("Q", [P, TILES], F32)
        hs_part = sb("hs_part", [P, N // 512], F32)
        st = sb("st", [P, 16], F32)
        den_r = sb("den_r", [P, 3 * SUB_G], F32)
        flags = sb("flags", [P, LAYERS], F32)
        one_row = sb("one_row", [1, P], F32)
        neg1, K0, K08, nK0, dmax, hsum, gcur, ngcur, ogcur, k0s = (st[:, i:i + 1] for i in range(10))
        ps = ctx.enter_context(nc.psum_tensor("ps", [P, 8 * 512], F32))

        def bank(i, n, k=1):
            return ps[:, i * 512:i * 512 + n]

        x_in_s, key_in, val_in, w_in_s, consts = (sem(n) for n in ("x_in", "key_in", "val_in", "w_in", "consts"))
        dve_pro, key_split, wx_ready = sem("dve_pro"), sem("key_split"), sem("wx_ready")
        ln_step, xc_ready, sq_ready, var_ready, std_ready, h_ready, tr_ready, hT_ready = (
            sem(n) for n in ("ln_step", "xc_ready", "sq_ready", "var_ready", "std_ready", "h_ready",
                             "tr_ready", "hT_ready"))
        g_ready, g_half, g_made, g_in = sem("g_ready"), sem("g_half"), sem("g_made"), sem("g_in")
        g_stored = [sem(f"g_stored{i}") for i in range(2)]
        adj_in = [sem(f"adj_in{i}") for i in range(3)]
        not_made, save_made = sem("not_made"), sem("save_made")
        saved = [sem(f"saved{i}") for i in range(2)]
        scores_ready, evac_done, max_done, part_ready, mT_ready, mc_ready, rep_ready, mb_ready, maxb_ready = (
            sem(n) for n in ("scores_ready", "evac_done", "max_done", "part_ready", "mT_ready", "mc_ready",
                             "rep_ready", "mb_ready", "maxb_ready"))
        sub_done, exp_done, av_done, rden_ready, num_taken = (
            sem(n) for n in ("sub_done", "exp_done", "av_done", "rden_ready", "num_taken"))
        pre_step, wcur_ready, wh_ready, wh_taken, s_ready, s_taken = (
            sem(n) for n in ("pre_step", "wcur_ready", "wh_ready", "wh_taken", "s_ready", "s_taken"))
        dmax_ready, dT_ready, k0_ready, kb_ready, k_ready, bq_ready, rlin_ready, r_ready, u_ready = (
            sem(n) for n in ("dmax_ready", "dT_ready", "k0_ready", "kb_ready", "k_ready", "bq_ready",
                             "rlin_ready", "r_ready", "u_ready"))
        hsrep_ready, sumb_ready = sem("hsrep_ready"), sem("sumb_ready")
        mask_in = [sem(f"mask_in{i}") for i in range(2)]
        z_ready, p_made, p_free, acc_free, fin_step, neg_ready, expo_ready, x_done = (
            sem(n) for n in ("z_ready", "p_made", "p_free", "acc_free", "fin_step", "neg_ready",
                             "expo_ready", "x_done"))
        out_done, idle = sem("out_done"), sem("idle")

        block = ctx.enter_context(nc.Block())

        def hold(engine, semaphore, count):
            engine.wait_ge(semaphore, count)
            engine.sem_inc(idle, 1)

        @block.sync
        def _(sp):
            sp.dma_start(X[:, :, :], x_in).then_inc(x_in_s, 16)
            sp.dma_start(third, inp_t).then_inc(key_in, 16)
            for i in range(4):
                sp.dma_start(Wraw[:, i, :], w_in[i]).then_inc(w_in_s, 16)
            for i in range(LAYERS):
                sp.dma_start(a_rows[:, i, :], a_in[i].to_broadcast([P, 2 * D])).then_inc(w_in_s, 16)
            sp.dma_start(U[:, :, 0:D], inp_nat).then_inc(val_in, 16)

            def load_adj(b, g):
                m = b * GROUPS + g
                if not isinstance(m, int) or m >= 3:
                    sp.wait_ge(not_made, m - 2)
                sp.dma_start(adjb[:, g % 3, :], adj_in_d[ds(b, 1), g].rearrange("o p w -> p (o w)")
                             ).then_inc(adj_in[g % 3], 16)

            def store_mask(b, s):
                sp.wait_ge(save_made, b * GROUPS + 3 * s + 3)
                sp.dma_start(mask_scr[ds(b, 1), s].rearrange("o p w -> p (o w)"), saveb[:, s % 2, :]
                             ).then_inc(saved[s % 2], 16)

            def load_g(b):
                sp.dma_start(G[:, ds((b % 2) * 2 * WA, 2 * WA)].bitcast(F32),
                             g_scr[ds(b, 1)].rearrange("o p w -> p (o w)")).then_inc(g_in, 16)

            for g in range(3):
                load_adj(0, g)
            for b in range(BLOCKS_A):
                sp.wait_ge(g_made, b + 1)
                sp.dma_start(g_scr[b], G[:, (b % 2) * 2 * WA:(b % 2 + 1) * 2 * WA].bitcast(F32)
                             ).then_inc(g_stored[b % 2], 16)
            for s in g_stored:
                sp.wait_ge(s, 16 * (BLOCKS_A // 2))
            load_g(0)

            def adj_block(b, first):
                for g in range(GROUPS):
                    if not (first and g < 3):
                        load_adj(b, g)
                    if g == 2 and not first:
                        store_mask(b - 1, 3)
                    if g in (5, 8, 11):
                        store_mask(b, (g - 5) // 3)
                    if g == 5 and not (isinstance(b, int) and b == BLOCKS_A - 1):
                        sp.wait_ge(scores_ready, b * PAIRS + 1)
                        load_g(b + 1)

            adj_block(0, True)
            with sp.Fori(1, BLOCKS_A - 1) as b:
                adj_block(b, False)
            adj_block(BLOCKS_A - 1, False)
            store_mask(BLOCKS_A - 1, 3)
            for s in saved:
                sp.wait_ge(s, 16 * BLOCKS_A * SAVES // 2)
            sp.wait_ge(not_made, BLOCKS_A * GROUPS)

            with sp.Fori(0, LAYERS * BLOCKS_G) as lb:
                with sp.Fori(lb % BLOCKS_G, lb % BLOCKS_G + 1) as q:
                    for s in range(SAVES):
                        hold(sp, p_made, (lb * SAVES + s) * SAVE + CREDIT - SAVE)
                        sp.dma_start(
                            maskb[:, s % 2].rearrange("p h k w -> p h (k w)"),
                            mask_scr.rearrange("(q h) s p w -> q s p h w", h=2)[ds(q, 1), s].rearrange(
                                "o p h w -> p (o h) w")).then_inc(mask_in[s % 2], 16)
            sp.wait_ge(x_done, LAYERS * BLOCKS_G)
            sp.dma_start(out_d, X[:, :, :]).then_inc(out_done, 16)
            sp.wait_ge(out_done, 16)

        @block.gpsimd
        def _(pool):
            pool.memset(identF[:, :], 0.0).then_inc(consts, 1)
            pool.memset(negI[:, :], 0.0).then_inc(consts, 1)
            pool.wait_ge(consts, 2)
            pool.affine_select(out=identF[:, :], in_=identF[:, :], compare_op=ALU.not_equal, fill=1.0,
                               base=0, pattern=[[-1, P]], channel_multiplier=1).then_inc(consts, 1)
            pool.affine_select(out=negI[:, :], in_=negI[:, :], compare_op=ALU.not_equal, fill=MASKED,
                               base=0, pattern=[[-1, P]], channel_multiplier=1).then_inc(consts, 1)
            pool.memset(neg1, -1.0).then_inc(consts, 1)
            pool.memset(one_row[:, :], 1.0).then_inc(consts, 1)
            for l in range(LAYERS):
                pool.memset(flags[:, l:l + 1], 1.0 if l == 1 else 0.0).then_inc(consts, 1)

        @block.tensor
        def _(pe):
            pe.wait_ge(consts, CONSTS)

            def transposes(k):
                for g in range(N // 512):
                    if (g * 4) % LN_CHUNK == 0:
                        pe.wait_ge(h_ready, k * LN_CHUNKS + g * 4 // LN_CHUNK + 1)
                    if g >= 2:
                        pe.wait_ge(hT_ready, k * (N // 512) + g - 1)
                    for i in range(4):
                        t = 4 * g + i
                        mm = pe.transpose(bank(g % 2, 512)[:, i * P:(i + 1) * P], h[:, t, :], identF[:, :])
                    mm.then_inc(tr_ready, 1)

            transposes(0)
            pe.wait_ge(w_in_s, 16 * (4 + LAYERS))
            for b in range(BLOCKS_A):
                pe.wait_ge(hT_ready, -(-(b + 1) * WA // 512))
                if b >= 2:
                    pe.wait_ge(g_made, b - 1)
                pe.matmul(bank(2 + b % 2, WA), Wraw[:, 0, :], hT[:, b * WA:(b + 1) * WA],
                          start=True, stop=True).then_inc(g_ready, 1)

            def gen(b, t):
                n = b * PAIRS + t
                if t == 0:
                    pe.wait_ge(g_in, 16 * (b + 1))
                if not isinstance(n, int) or n >= 2:
                    pe.wait_ge(evac_done, n - 1)
                if t % 2 == 0:
                    pe.wait_ge(not_made, b * GROUPS + t // 2 + 1)
                g_hi = G[:, ds((b % 2) * 2 * WA, WA)]
                g_lo = G[:, ds((b % 2) * 2 * WA + WA, WA)]
                for q in range(2):
                    o = bank(2 * (t % 2) + q, WA)
                    c = slice((2 * t + q) * P, (2 * t + q + 1) * P)
                    m = (2 * (t % 2) + q) * WA
                    pe.matmul(o, key_hi[:, c], g_hi, start=True, stop=False)
                    pe.matmul(o, key_hi[:, c], g_lo, start=False, stop=False)
                    pe.matmul(o, key_lo[:, c], g_hi, start=False, stop=False)
                    mm = pe.matmul(o, negI[:, :], notb[:, (t // 2) % 3, m:m + WA], start=False, stop=True)
                mm.then_inc(scores_ready, 1)

            def row_max(b):
                pe.wait_ge(part_ready, b + 1)
                for c in range(SUB_A):
                    mm = pe.transpose(bank(5, WA)[:, c * P:(c + 1) * P], part_max[:, c * P:(c + 1) * P],
                                      identF[:, :])
                mm.then_inc(mT_ready, 1)
                pe.wait_ge(rep_ready, b + 1)
                for c in range(SUB_A):
                    mm = pe.matmul(bank(6, WA)[:, c * P:(c + 1) * P], max_rep[:, c, :], identF[:, :],
                                   start=True, stop=True)
                mm.then_inc(mb_ready, 1)

            def av(b, t):
                pe.wait_ge(exp_done, b * PAIRS + t + 1)
                if t == 0 and not (isinstance(b, int) and b == 0):
                    pe.wait_ge(num_taken, b)
                for q in range(2):
                    for c in range(SUB_A):
                        mm = pe.matmul(bank(4, 512)[:, c * E:(c + 1) * E], S[:, 2 * t + q, c * P:(c + 1) * P],
                                       U[:, 2 * t + q, :], start=(t == 0 and q == 0 and c == 0),
                                       stop=(t == PAIRS - 1 and q == 1), skip_group_check=True)
                mm.then_inc(av_done, 1)

            pe.wait_ge(key_split, 2)
            for t in range(PAIRS):
                gen(0, t)
            row_max(0)
            pe.wait_ge(val_in, 16)
            pe.wait_ge(wx_ready, 1)
            with pe.Fori(0, BLOCKS_A - 1) as b:
                for t in range(PAIRS):
                    av(b, t)
                    gen(b + 1, t)
                row_max(b + 1)
            for t in range(PAIRS):
                av(BLOCKS_A - 1, t)

            with pe.Fori(0, LAYERS) as l:
                transposes(l + 1)
                pe.wait_ge(wcur_ready, l + 1)
                for c in range(TILES // 3):
                    pe.wait_ge(hT_ready, (l + 1) * (N // 512) + -(-(c + 1) * WA // 512))
                    if c >= 2:
                        pe.wait_ge(wh_taken, l * (TILES // 3) + c - 1)
                    for i in range(3):
                        t = 3 * c + i
                        mm = pe.matmul(bank(2 + c % 2, 512)[:, i * E:(i + 1) * E], hT[:, t * P:(t + 1) * P],
                                       Wcur[:, :], start=True, stop=True)
                    mm.then_inc(wh_ready, 1)
                    if c >= 2:
                        pe.wait_ge(s_taken, l * BLOCKS_A + c - 1)
                    pe.matmul(bank(4 + c % 2, WA), va1_rep[:, :], hT[:, c * WA:(c + 1) * WA],
                              start=True, stop=True).then_inc(s_ready, 1)
                pe.wait_ge(dmax_ready, l + 1)
                pe.transpose(ps[0:1, 6 * 512:6 * 512 + P], dmax, identF[:, :]).then_inc(dT_ready, 1)
                pe.wait_ge(k0_ready, l + 1)
                pe.matmul(bank(7, 1), one_row[:, :], k0s[0:1, :], start=True, stop=True).then_inc(kb_ready, 1)
                pe.wait_ge(hsrep_ready, l + 1)
                pe.wait_ge(k_ready, l + 1)
                pe.matmul(bank(7, D), hsum_rep, Wcur[:, 0:D], start=True, stop=True).then_inc(sumb_ready, 1)
                hold(pe, u_ready, (l + 1) * 2 * LN_CHUNKS)
                with pe.Fori(0, BLOCKS_G // 2) as qq:
                    for s in range(2):
                        q = qq * 2 + s
                        pe.wait_ge(acc_free, l * BLOCKS_G + q + 1)
                        for j in range(TILES):
                            pe.wait_ge(p_made, (l * BLOCKS_G + q) * TILES + j + 1 + CREDIT)
                            for c in range(SUB_G):
                                mm = pe.matmul(bank(2 * s + c // 3, 512)[:, (c % 3) * E:(c % 3 + 1) * E],
                                               pring[:, j % RING, c * P:(c + 1) * P], U[:, j, :],
                                               start=(j == 0 and c % 3 == 0), stop=(j == TILES - 1),
                                               skip_group_check=True)
                            mm.then_inc(p_free, 1)

        @block.scalar
        def _(act):
            def ln(k):
                for c in range(LN_CHUNKS):
                    act.wait_ge(xc_ready, k * LN_CHUNKS + c + 1)
                    cs = slice(c * LN_CHUNK, (c + 1) * LN_CHUNK)
                    act.activation(sq[:, cs, :], h[:, cs, :], ACT.Square).then_inc(sq_ready, 1)
                act.wait_ge(var_ready, k + 1)
                act.activation(rstd[:, :], var[:, :], ACT.Sqrt).then_inc(std_ready, 1)
                for g in range(N // 512):
                    act.wait_ge(tr_ready, k * (N // 512) + g + 1)
                    act.activation(hT[:, g * 512:(g + 1) * 512], bank(g % 2, 512), ACT.Copy,
                                   accum_out=hs_part[:, g:g + 1]).then_inc(hT_ready, 1)

            ln(0)

            def evac(b, t):
                n = b * PAIRS + t
                act.wait_ge(scores_ready, n + 1)
                if not (isinstance(b, int) and b == 0):
                    act.wait_ge(av_done, (b - 1) * PAIRS + t + 1)
                src = ps[:, 2 * (t % 2) * 512:(2 * (t % 2) + 2) * 512].rearrange("p (q w) -> p q w", q=2)
                act.activation(S[:, 2 * t:2 * t + 2, :], src[:, :, 0:WA], ACT.Copy).then_inc(evac_done, 1)

            def save(b, g):
                act.wait_ge(not_made, b * GROUPS + g + 1)
                s = g // 3
                if g % 3 == 0 and not (isinstance(b, int) and b == 0 and s < 2):
                    act.wait_ge(saved[s % 2], 16 * (b * 2 + s // 2))
                act.activation(saveb[:, s % 2, (g % 3) * GROUP * WA:(g % 3 + 1) * GROUP * WA], notb[:, g % 3, :],
                               ACT.Copy, scale=-1.0, bias=1.0).then_inc(save_made, 1)

            def exps(b, t):
                act.wait_ge(sub_done, b * PAIRS + t + 1)
                act.activation(S[:, 2 * t:2 * t + 2, :], S[:, 2 * t:2 * t + 2, :], ACT.Exp,
                               scale=1.0 / TEMPERATURE).then_inc(exp_done, 1)

            for t in range(PAIRS):
                evac(0, t)
                if t % 2 == 0:
                    save(0, t // 2)
            with act.Fori(0, BLOCKS_A - 1) as b:
                exps(b, 0)
                exps(b, 1)
                for t in range(PAIRS):
                    evac(b + 1, t)
                    if t % 2 == 0:
                        save(b + 1, t // 2)
                    if t + 2 < PAIRS:
                        exps(b, t + 2)
            for t in range(PAIRS):
                exps(BLOCKS_A - 1, t)

            with act.Fori(0, LAYERS) as l:
                ln(l + 1)
                for c in range(TILES // 3):
                    act.wait_ge(wh_ready, l * (TILES // 3) + c + 1)
                    act.activation(U[:, 3 * c:3 * c + 3, :], bank(2 + c % 2, 3 * E).rearrange("p (c k) -> p c k", k=E),
                                   ACT.Copy).then_inc(wh_taken, 1)
                    act.wait_ge(s_ready, l * BLOCKS_A + c + 1)
                    act.activation(R[:, c * WA:(c + 1) * WA], bank(4 + c % 2, WA), ACT.Copy).then_inc(s_taken, 1)
                act.wait_ge(k_ready, l + 1)
                act.activation(B[:, :], U[:, :, D], ACT.Exp, bias=nK0).then_inc(bq_ready, 1)
                act.activation(Q[:, :], U[:, :, D], ACT.Exp, bias=K08, scale=-(1.0 - SLOPE)).then_inc(bq_ready, 1)
                for c in range(BLOCKS_G):
                    act.wait_ge(rlin_ready, l * BLOCKS_G + c + 1)
                    act.activation(R[:, c * WG:(c + 1) * WG], R[:, c * WG:(c + 1) * WG], ACT.Exp,
                                   scale=-(1.0 - SLOPE)).then_inc(r_ready, 1)
                act.wait_ge(r_ready, (l + 1) * BLOCKS_G)
                act.wait_ge(bq_ready, 2 * (l + 1))

                def z(q, j):
                    n = (l * BLOCKS_G + q) * TILES + j
                    hold(act, p_made, n - RING + 1 + CREDIT)
                    act.activation(zring[:, j % RING, :], R[:, ds(q * WG, WG)], ACT.Relu, bias=neg1,
                                   scale=Q[:, j:j + 1]).then_inc(z_ready, 1)

                def exp_out(q):
                    act.wait_ge(neg_ready, l * BLOCKS_G + q + 1)
                    act.activation(exp_o, neg_o, ACT.Exp).then_inc(expo_ready, 1)

                for j in range(HEAD - 1):
                    z(0, j)
                with act.Fori(0, BLOCKS_G - 1) as q:
                    for j in range(HEAD - 1, TILES):
                        z(q, j)
                    for j in range(HEAD - 1):
                        z(q + 1, j)
                    exp_out(q)
                for j in range(HEAD - 1, TILES):
                    z(BLOCKS_G - 1, j)
                exp_out(BLOCKS_G - 1)

        @block.vector
        def _(dve):
            dve.sem_inc(p_made, CREDIT)
            dve.sem_inc(p_free, RING)
            dve.sem_inc(acc_free, 2)
            dve.wait_ge(consts, CONSTS)

            dve.wait_ge(w_in_s, 16 * (4 + LAYERS))
            pro = Tally(dve_pro, 0)
            for l in range(LAYERS):
                pro.inc(dve.tensor_copy(WX[:, l, 0:D], Wraw[:, 1 + l, :]))
                pro.inc(dve.tensor_tensor_reduce(w_dot, Wraw[:, 1 + l, :], a_rows[:, l, 0:D], 1.0, 0.0, ALU.mult,
                                                 ALU.add, va1[:, l:l + 1]))
                pro.wait(dve)
                pro.inc(dve.tensor_tensor_reduce(w_dot, Wraw[:, 1 + l, :], a_rows[:, l, D:2 * D], 1.0, 0.0, ALU.mult,
                                                 ALU.add, WX[:, l, D:E]))
                pro.wait(dve)
            dve.wait_ge(key_in, 16)
            dve.tensor_copy(key_hi[:, :], third).then_inc(key_split, 1)
            dve.wait_ge(key_split, 1)
            dve.tensor_tensor(key_lo[:, :], third, key_hi[:, :].bitcast(F32), ALU.subtract).then_inc(key_split, 1)
            dve.memset(U[:, :, D:E], 1.0).then_inc(wx_ready, 1)
            dve.wait_ge(x_in_s, 16)

            def ln(k):
                own = Tally(ln_step, k * LN_STEPS)
                for c in range(LN_CHUNKS):
                    cs = slice(c * LN_CHUNK, (c + 1) * LN_CHUNK)
                    own.inc(dve.tensor_reduce(mean[:, cs], X[:, cs, :], AX.X, ALU.add))
                    own.wait(dve)
                    own.inc(dve.tensor_scalar(mean[:, cs], mean[:, cs], 1.0 / D, None, ALU.mult))
                    own.wait(dve)
                    dve.tensor_tensor(h[:, cs, :], X[:, cs, :],
                                      mean[:, cs].unsqueeze(2).to_broadcast([P, LN_CHUNK, D]),
                                      ALU.subtract).then_inc(xc_ready, 1)
                for c in range(LN_CHUNKS):
                    cs = slice(c * LN_CHUNK, (c + 1) * LN_CHUNK)
                    dve.wait_ge(sq_ready, k * LN_CHUNKS + c + 1)
                    own.inc(dve.tensor_reduce(var[:, cs], sq[:, cs, :], AX.X, ALU.add))
                own.wait(dve)
                dve.tensor_scalar(var[:, :], var[:, :], 1.0 / D, EPS, ALU.mult, ALU.add).then_inc(var_ready, 1)
                dve.wait_ge(std_ready, k + 1)
                own.inc(dve.reciprocal(rstd[:, :], rstd[:, :]))
                own.wait(dve)
                assert own.n == LN_STEPS
                for c in range(LN_CHUNKS):
                    cs = slice(c * LN_CHUNK, (c + 1) * LN_CHUNK)
                    dve.scalar_tensor_tensor(out=h[:, cs, :], in0=h[:, cs, :], scalar=0.0,
                                             in1=rstd[:, cs].unsqueeze(2).to_broadcast([P, LN_CHUNK, D]),
                                             op0=ALU.max, op1=ALU.mult).then_inc(h_ready, 1)

            ln(0)
            for b in range(BLOCKS_A):
                dve.wait_ge(g_ready, b + 1)
                if b >= 2:
                    dve.wait_ge(g_stored[b % 2], 16 * (b // 2))
                g_hi = G[:, (b % 2) * 2 * WA:(b % 2) * 2 * WA + WA]
                g_lo = G[:, (b % 2) * 2 * WA + WA:(b % 2 + 1) * 2 * WA]
                dve.tensor_copy(g_hi, bank(2 + b % 2, WA)).then_inc(g_half, 1)
                dve.wait_ge(g_half, b + 1)
                dve.tensor_tensor(g_lo, bank(2 + b % 2, WA), g_hi.bitcast(F32), ALU.subtract).then_inc(g_made, 1)

            def no_edge(b, g):
                m = b * GROUPS + g
                dve.wait_ge(adj_in[g % 3], 16 * (b * (GROUPS // 3) + g // 3 + 1))
                if not isinstance(m, int) or m >= 3:
                    dve.wait_ge(scores_ready, 2 * (m - 2))
                    dve.wait_ge(save_made, m - 2)
                dve.tensor_scalar(notb[:, g % 3, :], adjb[:, g % 3, :], 0, None, ALU.is_le).then_inc(not_made, 1)

            def keep_max(b, t):
                n = b * PAIRS + t
                dve.wait_ge(evac_done, n + 1)
                if t == 0:
                    dve.tensor_copy(run_max[:, :, :], S[:, 0:2, :]).then_inc(max_done, 1)
                else:
                    dve.wait_ge(max_done, n)
                    dve.tensor_tensor(run_max[:, :, :], run_max[:, :, :], S[:, 2 * t:2 * t + 2, :],
                                      ALU.max).then_inc(max_done, 1)

            def row_max(b):
                dve.wait_ge(max_done, (b + 1) * PAIRS)
                dve.tensor_tensor(part_max[:, :], run_max[:, 0, :], run_max[:, 1, :], ALU.max).then_inc(part_ready, 1)
                dve.wait_ge(mT_ready, b + 1)
                dve.tensor_reduce(max_c[:, :], bank(5, WA).rearrange("p (c w) -> p c w", w=P), AX.X,
                                  ALU.max).then_inc(mc_ready, 1)
                dve.wait_ge(mc_ready, b + 1)
                dve.tensor_copy(max_rep[:, :, :], max_c[:, :].unsqueeze(2).to_broadcast([P, SUB_A, P])
                                ).then_inc(rep_ready, 1)
                dve.wait_ge(mb_ready, b + 1)
                dve.tensor_copy(max_b[:, :], bank(6, WA)).then_inc(maxb_ready, 1)
                dve.wait_ge(maxb_ready, b + 1)

            def sub(b, t):
                dve.tensor_tensor(S[:, 2 * t:2 * t + 2, :], S[:, 2 * t:2 * t + 2, :],
                                  max_b[:, :].unsqueeze(1).to_broadcast([P, 2, WA]), ALU.subtract
                                  ).then_inc(sub_done, 1)

            def take(b):
                dve.wait_ge(av_done, (b + 1) * PAIRS)
                acc = bank(4, SUB_A * E).rearrange("p (c k) -> p c k", k=E)
                dve.reciprocal(den_r[:, 0:SUB_A], acc[:, :, D]).then_inc(rden_ready, 1)
                dve.wait_ge(rden_ready, b + 1)
                for c in range(SUB_A):
                    xs = X[:, ds(b * SUB_A + c, 1), :].rearrange("p o d -> p (o d)")
                    mm = dve.scalar_tensor_tensor(out=xs, in0=acc[:, c, 0:D], scalar=den_r[:, c:c + 1], in1=xs,
                                                  op0=ALU.mult, op1=ALU.add)
                mm.then_inc(num_taken, 1)

            no_edge(0, 0)
            for t in range(PAIRS):
                if t % 2 == 0 and t // 2 + 1 < GROUPS:
                    no_edge(0, t // 2 + 1)
                keep_max(0, t)
            row_max(0)
            with dve.Fori(0, BLOCKS_A - 1) as b:
                sub(b, 0)
                sub(b, 1)
                no_edge(b + 1, 0)
                sub(b, 2)
                for t in range(PAIRS):
                    if t % 2 == 0 and t // 2 + 1 < GROUPS:
                        no_edge(b + 1, t // 2 + 1)
                    if t + 3 < PAIRS:
                        sub(b, t + 3)
                    if t == PAIRS - 1:
                        take(b)
                    keep_max(b + 1, t)
                row_max(b + 1)
            for t in range(PAIRS):
                sub(BLOCKS_A - 1, t)
            take(BLOCKS_A - 1)
            dve.wait_ge(num_taken, BLOCKS_A)

            with dve.Fori(0, LAYERS) as l:
                ln(l + 1)
                PRE = 8
                own = Tally(pre_step, l * PRE)
                dve.wait_ge(hT_ready, (l + 2) * (N // 512))
                own.inc(dve.tensor_copy(va1_rep[:, :], va1[:, ds(l, 1)].to_broadcast([P, P])))
                own.inc(dve.tensor_copy(gcur, flags[:, ds(l, 1)]))
                own.wait(dve)
                own.inc(dve.tensor_scalar(ngcur, gcur, -1.0, None, ALU.mult))
                own.inc(dve.tensor_scalar(ogcur, gcur, -1.0, 1.0, ALU.mult, ALU.add))
                dve.tensor_copy(Wcur[:, :], WX[:, ds(l, 1), :].rearrange("p o k -> p (o k)")).then_inc(wcur_ready, 1)
                own.inc(dve.tensor_reduce(hsum, hs_part[:, :], AX.X, ALU.add))
                own.wait(dve)
                dve.tensor_copy(hsum_rep, hsum.to_broadcast([P, P])).then_inc(hsrep_ready, 1)
                dve.wait_ge(wh_taken, (l + 1) * (TILES // 3))
                dve.tensor_reduce(dmax, U[:, :, D], AX.X, ALU.max).then_inc(dmax_ready, 1)
                dve.wait_ge(dT_ready, l + 1)
                dve.tensor_reduce(k0s[0:1, :], ps[0:1, 6 * 512:6 * 512 + P], AX.X, ALU.max).then_inc(k0_ready, 1)
                dve.wait_ge(kb_ready, l + 1)
                own.inc(dve.tensor_copy(K0, bank(7, 1)))
                own.wait(dve)
                own.inc(dve.tensor_scalar(K08, K0, 1.0 - SLOPE, None, ALU.mult))
                own.wait(dve)
                dve.tensor_scalar(nK0, K0, -1.0, None, ALU.mult).then_inc(k_ready, 1)
                dve.wait_ge(s_taken, (l + 1) * BLOCKS_A)
                for c in range(BLOCKS_G):
                    rs = R[:, c * WG:(c + 1) * WG]
                    dve.tensor_scalar(rs, rs, K0, 0.0, ALU.add, ALU.max).then_inc(rlin_ready, 1)
                dve.wait_ge(sumb_ready, l + 1)
                own.inc(dve.tensor_copy(sum_b[:, :], bank(7, D)))
                dve.wait_ge(bq_ready, 2 * (l + 1))
                for c in range(LN_CHUNKS):
                    cs = slice(c * LN_CHUNK, (c + 1) * LN_CHUNK)
                    dve.tensor_tensor(U[:, cs, 0:D], U[:, cs, 0:D],
                                      B[:, cs].unsqueeze(2).to_broadcast([P, LN_CHUNK, D]),
                                      ALU.mult).then_inc(u_ready, 1)
                    dve.tensor_copy(U[:, cs, D], B[:, cs]).then_inc(u_ready, 1)
                own.wait(dve)
                assert own.n == PRE, own.n

                def weights(q, j):
                    n = (l * BLOCKS_G + q) * TILES + j
                    s = j // SAVE
                    if j % SAVE == 0:
                        dve.wait_ge(mask_in[s % 2], 16 * ((l * BLOCKS_G + q) * 2 + s // 2 + 1))
                    dve.wait_ge(z_ready, n + 1)
                    dve.wait_ge(p_free, n + 1)
                    two = "p (h w) -> p h w"
                    dve.scalar_tensor_tensor(out=pring[:, j % RING, :].rearrange(two, h=2),
                                             in0=zring[:, j % RING, :].rearrange(two, h=2), scalar=1.0,
                                             in1=maskb[:, s % 2, :, j % SAVE, :], op0=ALU.add, op1=ALU.mult
                                             ).then_inc(p_made, 1)

                FIN = 9
                def finish1(q):
                    fin = Tally(fin_step, (l * BLOCKS_G + q) * FIN)
                    dve.wait_ge(p_free, (l * BLOCKS_G + q + 1) * TILES + RING)
                    empty, den, inv = (den_r[:, i * SUB_G:(i + 1) * SUB_G] for i in range(3))
                    accs = [ps[:, ds((q % 2) * 1024 + i * 512, 3 * E)].rearrange("p (c k) -> p c k", k=E)
                            for i in range(2)]
                    for i in range(2):
                        fin.inc(dve.tensor_scalar(empty[:, 3 * i:3 * i + 3], accs[i][:, :, D], 0.0, None,
                                                  ALU.is_equal))
                    fin.wait(dve)
                    for i in range(2):
                        fin.inc(dve.scalar_tensor_tensor(out=den[:, 3 * i:3 * i + 3], in0=empty[:, 3 * i:3 * i + 3],
                                                         scalar=float(N), in1=accs[i][:, :, D], op0=ALU.mult,
                                                         op1=ALU.add))
                    fin.wait(dve)
                    fin.inc(dve.reciprocal(inv, den))
                    for c in range(SUB_G):
                        mm = dve.scalar_tensor_tensor(out=o_buf[:, c * D:(c + 1) * D], in0=sum_b[:, :],
                                                      scalar=empty[:, c:c + 1], in1=accs[c // 3][:, c % 3, 0:D],
                                                      op0=ALU.mult, op1=ALU.add)
                    mm.then_inc(acc_free, 1)
                    dve.wait_ge(acc_free, l * BLOCKS_G + q + 1 + 2)
                    fin.wait(dve)
                    six = "p (c d) -> p c d"
                    fin.inc(dve.tensor_tensor(o_buf.rearrange(six, d=D), o_buf.rearrange(six, d=D),
                                              inv.unsqueeze(2).to_broadcast([P, SUB_G, D]), ALU.mult))
                    fin.wait(dve)
                    dve.tensor_scalar(neg_o, o_buf, 0.0, None, ALU.min).then_inc(neg_ready, 1)
                    return fin

                def finish2(q, fin):
                    dve.wait_ge(expo_ready, l * BLOCKS_G + q + 1)
                    fin.inc(dve.tensor_scalar(exp_o, exp_o, gcur, ngcur, ALU.mult, ALU.add))
                    fin.wait(dve)
                    fin.inc(dve.scalar_tensor_tensor(out=exp_o, in0=neg_o, scalar=ogcur, in1=exp_o, op0=ALU.mult,
                                                     op1=ALU.add))
                    fin.wait(dve)
                    fin.inc(dve.scalar_tensor_tensor(out=o_buf, in0=o_buf, scalar=0.0, in1=exp_o, op0=ALU.max,
                                                     op1=ALU.add))
                    fin.wait(dve)
                    assert fin.n == FIN, fin.n
                    xs = X[:, ds(q * SUB_G, SUB_G), :]
                    dve.tensor_tensor(xs, xs, o_buf.rearrange("p (c d) -> p c d", d=D), ALU.add).then_inc(x_done, 1)

                for j in range(HEAD):
                    weights(0, j)
                with dve.Fori(0, BLOCKS_G - 1) as q:
                    for j in range(HEAD, TILES):
                        weights(q, j)
                    for j in range(HEAD):
                        weights(q + 1, j)
                        if j == 5:
                            fin = finish1(q)
                    finish2(q, fin)
                for j in range(HEAD, TILES):
                    weights(BLOCKS_G - 1, j)
                finish2(BLOCKS_G - 1, finish1(BLOCKS_G - 1))
                dve.wait_ge(x_done, (l + 1) * BLOCKS_G)


def kernel(x, adj, L0_gnn_input, L0_gnn_weight, L1_gnn_W, L1_gnn_a, L2_gnn_W, L2_gnn_a, L3_gnn_W, L3_gnn_a):
    import numpy as np
    import concourse.bacc as bacc
    from concourse.bass_utils import run_bass_kernel_spmd

    def rows(a):
        return np.ascontiguousarray(np.asarray(a).reshape(TILES, P, D).transpose(1, 0, 2))

    adj_t = np.ascontiguousarray(
        np.asarray(adj).reshape(BLOCKS_A, WA, GROUPS, GROUP, P).transpose(0, 2, 4, 3, 1)
    ).reshape(BLOCKS_A, GROUPS, P, GROUP * WA)
    arrays = {
        "x": rows(x), "adj": adj_t, "values": rows(L0_gnn_input),
        "keys": np.ascontiguousarray(np.asarray(L0_gnn_input).T),
        "w0": np.asarray(L0_gnn_weight), "w1": np.asarray(L1_gnn_W), "w2": np.asarray(L2_gnn_W),
        "w3": np.asarray(L3_gnn_W),
        "a1": np.asarray(L1_gnn_a).reshape(1, 2 * D), "a2": np.asarray(L2_gnn_a).reshape(1, 2 * D),
        "a3": np.asarray(L3_gnn_a).reshape(1, 2 * D),
    }
    nc = bacc.Bacc("TRN2", target_bir_lowering=False, num_devices=1, dynamic_dma_scratch_size=256)
    t = {n: nc.dram_tensor(n + "_dram", a.shape, mybir.dt.from_np(a.dtype), kind="ExternalInput").ap()
         for n, a in arrays.items()}
    out = nc.dram_tensor("out_dram", (P, TILES, D), F32, kind="ExternalOutput").ap()
    mask_scr = nc.dram_tensor("mask_scr", (BLOCKS_A, SAVES, P, SAVE * WA), U8, kind="Internal").ap()
    g_scr = nc.dram_tensor("g_scr", (BLOCKS_A, P, 2 * WA), F32, kind="Internal").ap()
    program(nc, t["x"], t["adj"], t["values"], t["keys"], [t[f"w{i}"] for i in range(4)],
            [t[f"a{i}"] for i in range(1, 4)], mask_scr, g_scr, out)
    r = run_bass_kernel_spmd(nc, [{n + "_dram": a for n, a in arrays.items()}], core_ids=[0])
    return r.results[0]["out_dram"].transpose(1, 0, 2).reshape(N, D)
```

```python
from contextlib import ExitStack

import concourse.bass as bass
from concourse import mybir

F32 = mybir.dt.float32
F32R = mybir.dt.float32r
BF16 = mybir.dt.bfloat16
I32 = mybir.dt.int32
U8 = mybir.dt.uint8
ALU = mybir.AluOpType
ACT = mybir.ActivationFunctionType
AX = mybir.AxisListType

P = 128
N = 6144
D = 128
TILES = N // P
LAYERS = 3
TEMPERATURE = 0.07
SLOPE = 0.2
EPS = 1e-5
MASKED = -2.0 ** 100

WA = 384
BLOCKS_A = N // WA
SUB_A = WA // P
PAIRS = TILES // 2
GROUP = 4
GROUPS = TILES // GROUP
SAVE = 12
SAVES = TILES // SAVE

WG = 2 * WA
BLOCKS_G = N // WG
SUB_G = WG // P
RING = 4
CREDIT = 13
E = D + 1
CHUNK = 12
CHUNKS = TILES // CHUNK
CONSTS = 6
SPREAD = 60.0
X_STEPS = [6, 8, 6]
QUERIES = 128
BLOCKS_X = N // QUERIES
ELU_LAYER = 1


class Tally:

    def __init__(self, sem, base):
        self.sem, self.base, self.n = sem, base, 0

    def inc(self, instruction):
        instruction.then_inc(self.sem, 1)
        self.n += 1

    def wait(self, engine):
        engine.wait_ge(self.sem, self.base + self.n)


def ds(start, size):
    return bass.ds(start, size)


def program(nc, x_in, adj_in_d, inp_nat, inp_t, w_in, a_in, mask_scr, g_scr, out_d):
    ctx = ExitStack()
    with ctx:
        def sb(name, shape, dt):
            return ctx.enter_context(nc.sbuf_tensor(name, shape, dt))

        def sem(name):
            return ctx.enter_context(nc.semaphore(name))

        arena = sb("arena", [P, TILES * WA], F32)
        S = arena[:, :].rearrange("p (t w) -> p t w", w=WA)
        third = [arena[:, i * N:(i + 1) * N] for i in range(3)]
        h_all = third[0]
        zring = arena[:, 0:RING * WG].rearrange("p (s w) -> p s w", w=WG)
        pring = arena[:, RING * WG:2 * RING * WG].rearrange("p (s w) -> p s w", w=WG)
        R_of = [third[2], third[1], third[2]]
        spare_of = [third[1], third[2], third[1]]
        key_hi = sb("key_hi", [P, N], F32R)
        key_lo = sb("key_lo", [P, N], F32R)
        maskb = key_hi[:, 0:2 * 2 * SAVE * WA // 4].bitcast(U8).rearrange(
            "p (s h k w) -> p s h k w", s=2, h=2, k=SAVE)
        maskx = key_lo[:, 0:TILES * QUERIES // 4].bitcast(U8).rearrange("p (t w) -> p t w", w=QUERIES)
        U0 = sb("U0", [P, TILES, E], F32)
        X = sb("X", [P, TILES, D], F32)
        ADJ, NOT, SAV = 3 * GROUP * WA, 3 * GROUP * WA // 2, 2 * SAVE * WA // 4
        stage = sb("stage", [P, ADJ + NOT + SAV], I32)
        adjb = stage[:, 0:ADJ].rearrange("p (s w) -> p s w", s=3)
        notb = stage[:, ADJ:ADJ + NOT].bitcast(BF16).rearrange("p (s w) -> p s w", s=3)
        saveb = stage[:, ADJ + NOT:ADJ + NOT + SAV].bitcast(U8).rearrange("p (s w) -> p s w", s=2)
        stagef = stage[:, :].bitcast(F32)
        U1 = stagef[:, 0:TILES * E].rearrange("p (t k) -> p t k", k=E)
        U_of = [U0, U1, U0]
        hT_blk, neg_o, exp_o = (stagef[:, TILES * E + i * WG:TILES * E + (i + 1) * WG] for i in range(3))
        Wraw = stagef[:, ADJ:ADJ + 4 * D].rearrange("p (l f) -> p l f", l=4)
        a_rows = stagef[:, ADJ + NOT:ADJ + NOT + LAYERS * 2 * D].rearrange("p (l f) -> p l f", l=LAYERS)
        w_dot = stagef[:, ADJ + NOT + LAYERS * 2 * D:ADJ + NOT + (LAYERS * 2 + 1) * D]
        G = sb("G", [P, 4 * WA], F32R)
        run_max = sb("run_max", [P, 2, WA], F32)
        o_buf = run_max[:, :, :].rearrange("p a w -> p (a w)")
        part_max = sb("part_max", [P, WA], F32)
        h_blk = sb("h_blk", [P, WG], F32)
        max_c = sb("max_c", [P, SUB_A], F32)
        identF = sb("identF", [P, P], F32)
        negI = sb("negI", [P, P], BF16)
        WX = sb("WX", [P, LAYERS, E], F32)
        va1 = sb("va1", [P, LAYERS], F32)
        sum_b = sb("sum_b", [P, D], F32)
        stats = sb("stats", [P, SUB_G, 6], F32)
        mv = sb("mv", [P, 2, SUB_G, 2], F32)
        var = sb("var", [P, 2, SUB_G], F32)
        rstd = sb("rstd", [P, 2, SUB_G], F32)
        B = sb("B", [P, TILES], F32)
        Q = sb("Q", [P, TILES], F32)
        hs_part = sb("hs_part", [P, N // WA], F32)
        st = sb("st", [P, 16], F32)
        den_r = sb("den_r", [P, 3 * SUB_G], F32)
        path = sb("path", [1, 1], I32)
        one_row = sb("one_row", [1, P], F32)
        neg1, K0, K08, nK0, dmax, dmin, hsum, k0s, k1s = (st[:, i:i + 1] for i in range(9))
        ps = ctx.enter_context(nc.psum_tensor("ps", [P, 8 * 512], F32))

        def bank(i, n, k=1):
            return ps[:, i * 512:i * 512 + n]

        x_in_s, key_in, val_in, w_in_s, consts = (sem(n) for n in ("x_in", "key_in", "val_in", "w_in", "consts"))
        dve_pro, key_split, wx_ready = sem("dve_pro"), sem("key_split"), sem("wx_ready")
        stat_ready, aggr_ready, var_ready, std_ready, rc_ready, h_ready, tr_ready, hT_ready = (
            sem(n) for n in ("stat_ready", "aggr_ready", "var_ready", "std_ready", "rc_ready", "h_ready",
                             "tr_ready", "hT_ready"))
        g_ready, g_half, g_made, g_in = sem("g_ready"), sem("g_half"), sem("g_made"), sem("g_in")
        g_stored = [sem(f"g_stored{i}") for i in range(2)]
        adj_in = [sem(f"adj_in{i}") for i in range(3)]
        not_made, save_made = sem("not_made"), sem("save_made")
        saved = [sem(f"saved{i}") for i in range(2)]
        scores_ready, evac_done, max_done, part_ready, mT_ready, mc_ready, mb_ready = (
            sem(n) for n in ("scores_ready", "evac_done", "max_done", "part_ready", "mT_ready", "mc_ready",
                             "mb_ready"))
        sub_done, exp_done, av_done, rden_ready, num_taken = (
            sem(n) for n in ("sub_done", "exp_done", "av_done", "rden_ready", "num_taken"))
        pre_step, wh_ready, wh_taken, s_ready, s_taken = (
            sem(n) for n in ("pre_step", "wh_ready", "wh_taken", "s_ready", "s_taken"))
        dmm_ready, dT_ready, k0_ready, kb_ready, k_ready, path_ready, hsum_ready, sumb_ready = (
            sem(n) for n in ("dmm_ready", "dT_ready", "k0_ready", "kb_ready", "k_ready", "path_ready",
                             "hsum_ready", "sumb_ready"))
        mask_in = [sem(f"mask_in{i}") for i in range(2)]
        bq_ready, rlin_ready, r_ready, u_ready, z_ready, p_made, p_free, acc_free, fin_step, neg_ready, expo_ready = (
            sem(n) for n in ("bq_ready", "rlin_ready", "r_ready", "u_ready", "z_ready", "p_made", "p_free",
                             "acc_free", "fin_step", "neg_ready", "expo_ready"))
        x_mask_in, x_ones, x_step, x_masked, x_part, x_mT, x_mc, x_mb, x_sub, x_exp, x_av, x_neg, x_eo = (
            sem(n) for n in ("x_mask_in", "x_ones", "x_step", "x_masked", "x_part", "x_mT", "x_mc", "x_mb",
                             "x_sub", "x_exp", "x_av", "x_neg", "x_eo"))
        x_done, elu_step = sem("x_done"), sem("elu_step")
        out_done, idle = sem("out_done"), sem("idle")

        block = ctx.enter_context(nc.Block())

        def hold(engine, semaphore, count):
            engine.wait_ge(semaphore, count)
            engine.sem_inc(idle, 1)

        def either_path(engine, l, general, factored):
            engine.wait_ge(path_ready, l + 1)
            choice = engine.value_load(path[0:1, 0:1], min_val=0, max_val=1)
            with engine.If(choice == 1):
                general(l)
            with engine.Else():
                factored(l)

        @block.sync
        def _(sp):
            sp.dma_start(X[:, :, :], x_in).then_inc(x_in_s, 16)
            sp.dma_start(third[2], inp_t).then_inc(key_in, 16)
            for i in range(4):
                sp.dma_start(Wraw[:, i, :], w_in[i]).then_inc(w_in_s, 16)
            for i in range(LAYERS):
                sp.dma_start(a_rows[:, i, :], a_in[i].to_broadcast([P, 2 * D])).then_inc(w_in_s, 16)
            sp.dma_start(U0[:, :, 0:D], inp_nat).then_inc(val_in, 16)

            def load_adj(b, g):
                m = b * GROUPS + g
                if not isinstance(m, int) or m >= 3:
                    sp.wait_ge(not_made, m - 2)
                sp.dma_start(adjb[:, g % 3, :], adj_in_d[ds(b, 1), g].rearrange("o p w -> p (o w)")
                             ).then_inc(adj_in[g % 3], 16)

            def store_mask(b, s):
                sp.wait_ge(save_made, b * GROUPS + 3 * s + 3)
                sp.dma_start(mask_scr[ds(b, 1), s].rearrange("o p w -> p (o w)"), saveb[:, s % 2, :]
                             ).then_inc(saved[s % 2], 16)

            def load_g(b):
                sp.dma_start(G[:, ds((b % 2) * 2 * WA, 2 * WA)].bitcast(F32),
                             g_scr[ds(b, 1)].rearrange("o p w -> p (o w)")).then_inc(g_in, 16)

            for g in range(3):
                load_adj(0, g)
            for b in range(BLOCKS_A):
                sp.wait_ge(g_made, b + 1)
                sp.dma_start(g_scr[b], G[:, (b % 2) * 2 * WA:(b % 2 + 1) * 2 * WA].bitcast(F32)
                             ).then_inc(g_stored[b % 2], 16)
            for s in g_stored:
                sp.wait_ge(s, 16 * (BLOCKS_A // 2))
            load_g(0)

            def adj_block(b, first):
                for g in range(GROUPS):
                    if not (first and g < 3):
                        load_adj(b, g)
                    if g == 2 and not first:
                        store_mask(b - 1, 3)
                    if g in (5, 8, 11):
                        store_mask(b, (g - 5) // 3)
                    if g == 5 and not (isinstance(b, int) and b == BLOCKS_A - 1):
                        sp.wait_ge(scores_ready, b * PAIRS + 1)
                        load_g(b + 1)

            adj_block(0, True)
            with sp.Fori(1, BLOCKS_A - 1) as b:
                adj_block(b, False)
            adj_block(BLOCKS_A - 1, False)
            store_mask(BLOCKS_A - 1, 3)
            for s in saved:
                sp.wait_ge(s, 16 * BLOCKS_A * SAVES // 2)
            sp.wait_ge(not_made, BLOCKS_A * GROUPS)

            def factored(l):
                sp.sem_inc(x_mask_in, 16 * BLOCKS_X * SAVES)
                with sp.Fori(0, BLOCKS_G) as q:
                    for s in range(SAVES):
                        hold(sp, p_made, ((l * BLOCKS_G + q) * SAVES + s) * SAVE + CREDIT - SAVE)
                        sp.dma_start(
                            maskb[:, s % 2].bitcast(U8).rearrange("p h k w -> p h (k w)"),
                            mask_scr.rearrange("(q h) s p w -> q s p h w", h=2)[ds(q, 1), s].rearrange(
                                "o p h w -> p (o h) w")).then_inc(mask_in[s % 2], 16)

            def general(l):
                for s in mask_in:
                    sp.sem_inc(s, 16 * BLOCKS_G * SAVES // 2)
                with sp.Fori(0, BLOCKS_A) as b:
                    for c in range(SUB_A):
                        hold(sp, x_masked, l * BLOCKS_X + b * SUB_A + c + 1)
                        for s in range(SAVES):
                            src = mask_scr[ds(b, 1), s].rearrange("o p (k w) -> p (o k) w", w=WA)
                            dma = sp.dma_start(maskx[:, s * SAVE:(s + 1) * SAVE, :],
                                               src[:, :, c * QUERIES:(c + 1) * QUERIES])
                            dma.then_inc(x_mask_in, 16)

            for l in range(LAYERS):
                either_path(sp, l, general, factored)
            sp.wait_ge(x_done, LAYERS * BLOCKS_G)
            sp.dma_start(out_d, X[:, :, :]).then_inc(out_done, 16)
            sp.wait_ge(out_done, 16)

        @block.gpsimd
        def _(pool):
            pool.memset(identF[:, :], 0.0).then_inc(consts, 1)
            pool.memset(negI[:, :], 0.0).then_inc(consts, 1)
            pool.wait_ge(consts, 2)
            pool.affine_select(out=identF[:, :], in_=identF[:, :], compare_op=ALU.not_equal, fill=1.0,
                               base=0, pattern=[[-1, P]], channel_multiplier=1).then_inc(consts, 1)
            pool.affine_select(out=negI[:, :], in_=negI[:, :], compare_op=ALU.not_equal, fill=MASKED,
                               base=0, pattern=[[-1, P]], channel_multiplier=1).then_inc(consts, 1)
            pool.memset(neg1, -1.0).then_inc(consts, 1)
            pool.memset(one_row[:, :], 1.0).then_inc(consts, 1)

        @block.tensor
        def _(pe):
            pe.wait_ge(consts, CONSTS)

            def transposes(k, q, h):
                n = k * BLOCKS_G + q
                pe.wait_ge(h_ready, n + 1)
                for i in range(2):
                    for c in range(3 * i, 3 * i + 3):
                        mm = pe.transpose(bank(4 + i, 512)[:, (c % 3) * P:(c % 3 + 1) * P],
                                          h[:, c * D:(c + 1) * D], identF[:, :])
                    mm.then_inc(tr_ready, 1)

            def project(l, q, hT):
                for i in range(2):
                    pe.wait_ge(hT_ready, 2 * ((l + 1) * BLOCKS_G + q) + i + 1)
                    half = hT[:, i * WA:(i + 1) * WA]
                    for c in range(3):
                        mm = pe.matmul(bank(6 + i, 512)[:, c * E:(c + 1) * E], half[:, c * P:(c + 1) * P],
                                       WX[:, l, :], start=True, stop=True)
                    mm.then_inc(wh_ready, 1)
                    pe.matmul(bank(4 + i, WA), va1[:, l:l + 1].to_broadcast([P, P]), half,
                              start=True, stop=True).then_inc(s_ready, 1)

            def g_rows(q):
                for i in range(2):
                    b = 2 * q + i
                    pe.wait_ge(hT_ready, b + 1)
                    if b >= 2:
                        pe.wait_ge(g_made, b - 1)
                    pe.matmul(bank(2 + i, WA), Wraw[:, 0, :], third[1][:, b * WA:(b + 1) * WA],
                              start=True, stop=True).then_inc(g_ready, 1)

            for q in range(BLOCKS_G + 1):
                if q < BLOCKS_G:
                    if q >= 1:
                        pe.wait_ge(hT_ready, 2 * q)
                    transposes(0, q, h_all[:, q * WG:(q + 1) * WG])
                if q == 0:
                    pe.wait_ge(w_in_s, 16 * (4 + LAYERS))
                else:
                    g_rows(q - 1)

            def gen(b, t):
                n = b * PAIRS + t
                if t == 0:
                    pe.wait_ge(g_in, 16 * (b + 1))
                if not isinstance(n, int) or n >= 3:
                    pe.wait_ge(evac_done, n - 2)
                if t % 2 == 0:
                    pe.wait_ge(not_made, b * GROUPS + t // 2 + 1)
                g_hi = G[:, ds((b % 2) * 2 * WA, WA)]
                g_lo = G[:, ds((b % 2) * 2 * WA + WA, WA)]
                for q in range(2):
                    o = bank(2 * (t % 3) + q, WA)
                    c = slice((2 * t + q) * P, (2 * t + q + 1) * P)
                    m = (2 * (t % 2) + q) * WA
                    pe.matmul(o, key_hi[:, c], g_hi, start=True, stop=False)
                    pe.matmul(o, key_hi[:, c], g_lo, start=False, stop=False)
                    pe.matmul(o, key_lo[:, c], g_hi, start=False, stop=False)
                    mm = pe.matmul(o, negI[:, :], notb[:, (t // 2) % 3, m:m + WA], start=False, stop=True)
                mm.then_inc(scores_ready, 1)

            def row_max_t(b):
                pe.wait_ge(part_ready, b + 1)
                for c in range(SUB_A):
                    mm = pe.transpose(bank(7, WA)[:, c * P:(c + 1) * P], part_max[:, c * P:(c + 1) * P],
                                      identF[:, :])
                mm.then_inc(mT_ready, 1)

            def row_max_b(b):
                pe.wait_ge(mc_ready, b + 1)
                for c in range(SUB_A):
                    mm = pe.matmul(bank(7, WA)[:, c * P:(c + 1) * P], max_c[:, c:c + 1].to_broadcast([P, P]),
                                   identF[:, :], start=True, stop=True)
                mm.then_inc(mb_ready, 1)

            def av(b, t):
                pe.wait_ge(exp_done, b * PAIRS + t + 1)
                if t == 0 and not (isinstance(b, int) and b == 0):
                    pe.wait_ge(num_taken, b)
                for q in range(2):
                    for c in range(SUB_A):
                        mm = pe.matmul(bank(6, 512)[:, c * E:(c + 1) * E], S[:, 2 * t + q, c * P:(c + 1) * P],
                                       U0[:, 2 * t + q, :], start=(t == 0 and q == 0 and c == 0),
                                       stop=(t == PAIRS - 1 and q == 1), skip_group_check=True)
                mm.then_inc(av_done, 1)

            pe.wait_ge(key_split, 2)
            for t in range(PAIRS):
                gen(0, t)
            row_max_t(0)
            row_max_b(0)
            pe.wait_ge(val_in, 16)
            pe.wait_ge(wx_ready, 1)

            def step_a(b):
                gen(b + 1, 0)
                gen(b + 1, 1)
                for t in range(PAIRS):
                    av(b, t)
                    if t + 2 < PAIRS:
                        gen(b + 1, t + 2)
                    if t == PAIRS - 2:
                        row_max_t(b + 1)
                row_max_b(b + 1)

            with pe.Fori(0, BLOCKS_A - 2) as b:
                step_a(b)
            step_a(BLOCKS_A - 2)
            for t in range(PAIRS):
                av(BLOCKS_A - 1, t)

            def all_blocks(l, hT):
                for q in range(BLOCKS_G + 1):
                    if q < BLOCKS_G:
                        if q >= 1:
                            pe.wait_ge(s_taken, 2 * (l * BLOCKS_G + q) - 2)
                            pe.wait_ge(hT_ready, 2 * ((l + 1) * BLOCKS_G + q))
                        transposes(l + 1, q, h_all[:, q * WG:(q + 1) * WG])
                    if q >= 1:
                        project_late(l, q - 1, hT[:, (q - 1) * WG:q * WG])

            def project_late(l, q, hT):
                if q >= 1:
                    pe.wait_ge(wh_taken, 2 * (l * BLOCKS_G + q))
                    pe.wait_ge(s_taken, 2 * (l * BLOCKS_G + q))
                if q + 1 < BLOCKS_G:
                    pe.wait_ge(hT_ready, 2 * ((l + 1) * BLOCKS_G + q + 2))
                project(l, q, hT)

            def choose(l):
                pe.wait_ge(dmm_ready, l + 1)
                pe.transpose(ps[0:1, 6 * 512:6 * 512 + P], dmax, identF[:, :])
                pe.transpose(ps[0:1, 6 * 512 + P:6 * 512 + 2 * P], dmin, identF[:, :]).then_inc(dT_ready, 1)
                pe.wait_ge(k0_ready, l + 1)
                pe.matmul(bank(7, 1), one_row[:, :], k0s[0:1, :], start=True, stop=True).then_inc(kb_ready, 1)
                pe.wait_ge(hsum_ready, l + 1)
                pe.wait_ge(k_ready, l + 1)
                pe.matmul(bank(7, D), hsum.to_broadcast([P, P]), WX[:, l, 0:D],
                          start=True, stop=True).then_inc(sumb_ready, 1)

            def factored(l):
                for s in (x_mT, x_mb, x_av):
                    pe.sem_inc(s, BLOCKS_X)
                pe.wait_ge(sumb_ready, l + 1)

                def sums(q, s, j):
                    pe.wait_ge(p_made, (l * BLOCKS_G + q) * TILES + j + 1 + CREDIT)
                    for c in range(SUB_G):
                        mm = pe.matmul(bank(2 * s + c // 3, 512)[:, (c % 3) * E:(c % 3 + 1) * E],
                                       pring[:, j % RING, c * P:(c + 1) * P], U_of[l][:, j, :],
                                       start=(j == 0 and c % 3 == 0), stop=(j == TILES - 1),
                                       skip_group_check=True)
                    mm.then_inc(p_free, 1)

                def block_g(q, s, last):
                    pe.wait_ge(acc_free, l * BLOCKS_G + q + 1)
                    for j in range(TILES):
                        if isinstance(q, int) and q == 0 and j % CHUNK == 0:
                            pe.wait_ge(u_ready, 2 * (l * CHUNKS + j // CHUNK + 1))
                        if l + 1 < LAYERS and last is not None:
                            if j == 22:
                                transposes(l + 2, last, h_blk[:, :])
                            if j == 28:
                                project(l + 1, last, hT_blk)
                        sums(q, s, j)

                block_g(0, 0, None)
                block_g(1, 1, 0)
                with pe.Fori(1, BLOCKS_G // 2) as qq:
                    for s in range(2):
                        block_g(qq * 2 + s, s, qq * 2 + s - 1)
                if l + 1 < LAYERS:
                    transposes(l + 2, BLOCKS_G - 1, h_blk[:, :])
                    project(l + 1, BLOCKS_G - 1, hT_blk)

            def general(l):
                pe.sem_inc(p_free, BLOCKS_G * TILES)
                pe.wait_ge(x_ones, 2 * (l + 1))
                pe.wait_ge(sumb_ready, l + 1)
                with pe.Fori(0, BLOCKS_X) as b:
                    n = l * BLOCKS_X + b
                    pe.wait_ge(x_part, n + 1)
                    pe.transpose(bank(7, P), part_max[:, 0:P], identF[:, :]).then_inc(x_mT, 1)
                    pe.wait_ge(x_mc, n + 1)
                    pe.matmul(bank(7, P), max_c[:, 0:1].to_broadcast([P, P]), identF[:, :],
                              start=True, stop=True).then_inc(x_mb, 1)
                    pe.wait_ge(x_exp, n + 1)
                    for j in range(TILES):
                        mm = pe.matmul(bank(6, E), h_all[:, j * QUERIES:(j + 1) * QUERIES], U_of[l][:, j, :],
                                       start=(j == 0), stop=(j == TILES - 1))
                    mm.then_inc(x_av, 1)
                if l + 1 < LAYERS:
                    all_blocks(l + 1, spare_of[l + 1])

            all_blocks(0, third[1])
            for l in range(LAYERS):
                choose(l)
                either_path(pe, l, general, factored)

        @block.scalar
        def _(act):
            def roots(k, q, slot):
                act.wait_ge(var_ready, k * BLOCKS_G + q + 1)
                act.activation(rstd[:, slot, :], var[:, slot, :], ACT.Sqrt).then_inc(std_ready, 1)

            def relu_T(k, q, hT):
                for i in range(2):
                    hold(act, tr_ready, 2 * (k * BLOCKS_G + q) + i + 1)
                    act.activation(hT[:, i * WA:(i + 1) * WA], bank(4 + i, WA), ACT.Relu,
                                   accum_out=hs_part[:, ds(2 * q + i, 1)]).then_inc(hT_ready, 1)

            def projected(l, q):
                for i in range(2):
                    hold(act, wh_ready, 2 * (l * BLOCKS_G + q) + i + 1)
                    act.activation(U_of[l][:, ds(6 * q + 3 * i, 3), :],
                                   bank(6 + i, 3 * E).rearrange("p (c k) -> p c k", k=E), ACT.Copy
                                   ).then_inc(wh_taken, 1)
                    hold(act, s_ready, 2 * (l * BLOCKS_G + q) + i + 1)
                    act.activation(R_of[l][:, ds((2 * q + i) * WA, WA)], bank(4 + i, WA), ACT.Copy
                                   ).then_inc(s_taken, 1)

            def all_blocks(k, hT, l):
                for q in range(BLOCKS_G + 2):
                    if q < BLOCKS_G:
                        roots(k, q, q % 2)
                    if 1 <= q <= BLOCKS_G:
                        relu_T(k, q - 1, hT[:, (q - 1) * WG:q * WG])
                    if l is not None and q >= 2:
                        projected(l, q - 2)

            all_blocks(0, third[1], None)

            def evac(b, t):
                n = b * PAIRS + t
                act.wait_ge(max_done, n + 1)
                if not (isinstance(b, int) and b == 0):
                    act.wait_ge(av_done, (b - 1) * PAIRS + t + 1)
                src = ps[:, 2 * (t % 3) * 512:(2 * (t % 3) + 2) * 512].rearrange("p (q w) -> p q w", q=2)
                act.activation(S[:, 2 * t:2 * t + 2, :], src[:, :, 0:WA], ACT.Copy).then_inc(evac_done, 1)

            def save(b, g):
                act.wait_ge(not_made, b * GROUPS + g + 1)
                s = g // 3
                if g % 3 == 0 and not (isinstance(b, int) and b == 0 and s < 2):
                    act.wait_ge(saved[s % 2], 16 * (b * 2 + s // 2))
                act.activation(saveb[:, s % 2, (g % 3) * GROUP * WA:(g % 3 + 1) * GROUP * WA], notb[:, g % 3, :],
                               ACT.Copy, scale=-1.0, bias=1.0).then_inc(save_made, 1)

            def exps(b, t):
                act.wait_ge(sub_done, b * PAIRS + t + 1)
                act.activation(S[:, 2 * t:2 * t + 2, :], S[:, 2 * t:2 * t + 2, :], ACT.Exp,
                               scale=1.0 / TEMPERATURE).then_inc(exp_done, 1)

            for t in range(PAIRS):
                evac(0, t)
                if t % 2 == 0:
                    save(0, t // 2)
            def step_a(b):
                for t in range(3):
                    exps(b, t)
                for t in range(PAIRS):
                    evac(b + 1, t)
                    if t + 3 < PAIRS:
                        exps(b, t + 3)
                    if t % 2 == 0:
                        save(b + 1, t // 2)

            with act.Fori(0, BLOCKS_A - 2) as b:
                step_a(b)
            step_a(BLOCKS_A - 2)
            for t in range(PAIRS):
                exps(BLOCKS_A - 1, t)

            def factored(l):
                for s in (x_exp,) + ((x_eo,) if l == ELU_LAYER else ()):
                    act.sem_inc(s, BLOCKS_X)
                U, R = U_of[l], R_of[l]
                act.wait_ge(k_ready, l + 1)
                act.activation(B[:, :], U[:, :, D], ACT.Exp, bias=nK0).then_inc(bq_ready, 1)
                act.activation(Q[:, :], U[:, :, D], ACT.Exp, bias=K08, scale=-(1.0 - SLOPE)).then_inc(bq_ready, 1)

                def row_factor(q):
                    hold(act, rlin_ready, l * BLOCKS_G + q + 1)
                    act.activation(R[:, ds(q * WG, WG)], R[:, ds(q * WG, WG)], ACT.Exp,
                                   scale=-(1.0 - SLOPE)).then_inc(r_ready, 1)

                def z(q, j):
                    n = (l * BLOCKS_G + q) * TILES + j
                    hold(act, p_made, n - RING + 1 + CREDIT)
                    act.activation(zring[:, j % RING, :], R[:, ds(q * WG, WG)], ACT.Relu, bias=neg1,
                                   scale=Q[:, j:j + 1]).then_inc(z_ready, 1)

                def exp_out(q):
                    act.wait_ge(neg_ready, q + 1)
                    act.activation(exp_o, neg_o, ACT.Exp).then_inc(expo_ready, 1)

                def block_g(q, last, more):
                    act.wait_ge(r_ready, l * BLOCKS_G + q + 1)
                    for j in range(TILES):
                        if last is not None:
                            if j == 10 and l == ELU_LAYER:
                                exp_out(last)
                            if l + 1 < LAYERS:
                                if j == 20:
                                    roots(l + 2, last, 0)
                                if j == 32:
                                    relu_T(l + 2, last, hT_blk)
                                if j == 38:
                                    projected(l + 1, last)
                        if j == 42 and more:
                            row_factor(q + 1)
                        z(q, j)

                row_factor(0)
                act.wait_ge(bq_ready, 2 * (l + 1))
                block_g(0, None, True)
                with act.Fori(1, BLOCKS_G - 1) as q:
                    block_g(q, q - 1, True)
                block_g(BLOCKS_G - 1, BLOCKS_G - 2, False)
                if l == ELU_LAYER:
                    exp_out(BLOCKS_G - 1)
                if l + 1 < LAYERS:
                    roots(l + 2, BLOCKS_G - 1, 0)
                    relu_T(l + 2, BLOCKS_G - 1, hT_blk)
                    projected(l + 1, BLOCKS_G - 1)

            def general(l):
                act.sem_inc(bq_ready, 2)
                act.sem_inc(r_ready, BLOCKS_G)
                act.sem_inc(z_ready, BLOCKS_G * TILES)
                if l == ELU_LAYER:
                    act.sem_inc(expo_ready, BLOCKS_G)
                with act.Fori(0, BLOCKS_X) as b:
                    act.wait_ge(x_sub, l * BLOCKS_X + b + 1)
                    act.activation(h_all, h_all, ACT.Exp).then_inc(x_exp, 1)
                    if l == ELU_LAYER:
                        act.wait_ge(x_neg, b + 1)
                        act.activation(exp_o[:, 0:D], neg_o[:, 0:D], ACT.Exp).then_inc(x_eo, 1)
                if l + 1 < LAYERS:
                    all_blocks(l + 2, spare_of[l + 1], l + 1)

            all_blocks(1, third[1], 0)
            for l in range(LAYERS):
                either_path(act, l, general, factored)

        @block.vector
        def _(dve):
            dve.sem_inc(p_made, CREDIT)
            dve.sem_inc(p_free, RING)
            dve.sem_inc(acc_free, 2)
            dve.sem_inc(x_masked, 1)
            dve.wait_ge(consts, CONSTS)

            dve.wait_ge(w_in_s, 16 * (4 + LAYERS))
            pro = Tally(dve_pro, 0)
            for l in range(LAYERS):
                pro.inc(dve.tensor_copy(WX[:, l, 0:D], Wraw[:, 1 + l, :]))
                pro.inc(dve.tensor_tensor_reduce(w_dot, Wraw[:, 1 + l, :], a_rows[:, l, 0:D], 1.0, 0.0, ALU.mult,
                                                 ALU.add, va1[:, l:l + 1]))
                pro.wait(dve)
                pro.inc(dve.tensor_tensor_reduce(w_dot, Wraw[:, 1 + l, :], a_rows[:, l, D:2 * D], 1.0, 0.0, ALU.mult,
                                                 ALU.add, WX[:, l, D:E]))
                pro.wait(dve)
            dve.wait_ge(key_in, 16)
            dve.tensor_copy(key_hi[:, :], third[2]).then_inc(key_split, 1)
            dve.wait_ge(key_split, 1)
            dve.tensor_tensor(key_lo[:, :], third[2], key_hi[:, :].bitcast(F32), ALU.subtract).then_inc(key_split, 1)
            dve.memset(U0[:, :, D:E], 1.0).then_inc(wx_ready, 1)
            dve.wait_ge(x_in_s, 16)

            def moments(k, q, slot):
                n = k * BLOCKS_G + q
                for c in range(SUB_G):
                    xs = X[:, ds(q * SUB_G + c, 1), :].rearrange("p o d -> p (o d)")
                    mm = dve.bn_stats(stats[:, c, :], xs)
                mm.then_inc(stat_ready, 1)
                hold(dve, stat_ready, n + 1)
                for c in range(SUB_G):
                    mm = dve.bn_aggr(mv[:, slot, c, :], stats[:, c, :])
                mm.then_inc(aggr_ready, 1)
                dve.wait_ge(aggr_ready, n + 1)
                dve.tensor_scalar(var[:, slot, :], mv[:, slot, :, 1], EPS, None, ALU.add).then_inc(var_ready, 1)

            def normalize(k, q, slot, h):
                n = k * BLOCKS_G + q
                dve.wait_ge(std_ready, n + 1)
                dve.reciprocal(rstd[:, slot, :], rstd[:, slot, :]).then_inc(rc_ready, 1)
                dve.wait_ge(rc_ready, n + 1)
                for c in range(SUB_G):
                    xs = X[:, ds(q * SUB_G + c, 1), :].rearrange("p o d -> p (o d)")
                    mm = dve.tensor_scalar(h[:, c * D:(c + 1) * D], xs, mv[:, slot, c, 0:1],
                                           rstd[:, slot, c:c + 1], ALU.subtract, ALU.mult)
                mm.then_inc(h_ready, 1)

            def split_g(q):
                for b in (2 * q, 2 * q + 1):
                    dve.wait_ge(g_ready, b + 1)
                    if b >= 2:
                        dve.wait_ge(g_stored[b % 2], 16 * (b // 2))
                    g_hi = G[:, (b % 2) * 2 * WA:(b % 2) * 2 * WA + WA]
                    g_lo = G[:, (b % 2) * 2 * WA + WA:(b % 2 + 1) * 2 * WA]
                    dve.tensor_copy(g_hi, bank(2 + b % 2, WA)).then_inc(g_half, 1)
                    dve.wait_ge(g_half, b + 1)
                    dve.tensor_tensor(g_lo, bank(2 + b % 2, WA), g_hi.bitcast(F32), ALU.subtract
                                      ).then_inc(g_made, 1)

            def all_blocks(k):
                for q in range(BLOCKS_G + 3):
                    if q < BLOCKS_G:
                        moments(k, q, q % 2)
                    if 1 <= q <= BLOCKS_G:
                        normalize(k, q - 1, (q - 1) % 2, h_all[:, (q - 1) * WG:q * WG])
                    if k == 0 and q >= 3:
                        split_g(q - 3)

            all_blocks(0)

            def no_edge(b, g):
                m = b * GROUPS + g
                dve.wait_ge(adj_in[g % 3], 16 * (b * (GROUPS // 3) + g // 3 + 1))
                if not isinstance(m, int) or m >= 3:
                    dve.wait_ge(scores_ready, 2 * (m - 2))
                    dve.wait_ge(save_made, m - 2)
                dve.tensor_scalar(notb[:, g % 3, :], adjb[:, g % 3, :], 0, None, ALU.is_le).then_inc(not_made, 1)

            def keep_max(b, t):
                n = b * PAIRS + t
                dve.wait_ge(scores_ready, n + 1)
                src = ps[:, 2 * (t % 3) * 512:(2 * (t % 3) + 2) * 512].rearrange("p (q w) -> p q w", q=2)[:, :, 0:WA]
                if t == 0:
                    dve.tensor_copy(run_max[:, :, :], src).then_inc(max_done, 1)
                else:
                    dve.wait_ge(max_done, n)
                    dve.tensor_tensor(run_max[:, :, :], run_max[:, :, :], src, ALU.max).then_inc(max_done, 1)

            def row_max(b):
                dve.wait_ge(max_done, (b + 1) * PAIRS)
                dve.tensor_tensor(part_max[:, :], run_max[:, 0, :], run_max[:, 1, :], ALU.max).then_inc(part_ready, 1)
                dve.wait_ge(mT_ready, b + 1)
                dve.tensor_reduce(max_c[:, :], bank(7, WA).rearrange("p (c w) -> p c w", w=P), AX.X,
                                  ALU.max).then_inc(mc_ready, 1)

            def sub(b, t):
                if t == 0:
                    dve.wait_ge(mb_ready, b + 1)
                    dve.wait_ge(evac_done, (b + 1) * PAIRS)
                dve.tensor_tensor(S[:, 2 * t:2 * t + 2, :], S[:, 2 * t:2 * t + 2, :],
                                  bank(7, WA).unsqueeze(1).to_broadcast([P, 2, WA]), ALU.subtract
                                  ).then_inc(sub_done, 1)

            def take(b):
                dve.wait_ge(av_done, (b + 1) * PAIRS)
                acc = bank(6, SUB_A * E).rearrange("p (c k) -> p c k", k=E)
                dve.reciprocal(den_r[:, 0:SUB_A], acc[:, :, D]).then_inc(rden_ready, 1)
                dve.wait_ge(rden_ready, b + 1)
                for c in range(SUB_A):
                    xs = X[:, ds(b * SUB_A + c, 1), :].rearrange("p o d -> p (o d)")
                    mm = dve.scalar_tensor_tensor(out=xs, in0=acc[:, c, 0:D], scalar=den_r[:, c:c + 1], in1=xs,
                                                  op0=ALU.mult, op1=ALU.add)
                mm.then_inc(num_taken, 1)

            no_edge(0, 0)
            no_edge(0, 1)
            for t in range(PAIRS):
                keep_max(0, t)
                if t % 2 == 0:
                    g = t // 2 + 2
                    no_edge(g // GROUPS, g % GROUPS)
            row_max(0)

            def step_a(b):
                sub(b, 0)
                sub(b, 1)
                keep_max(b + 1, 0)
                sub(b, 2)
                keep_max(b + 1, 1)
                sub(b, 3)
                sub(b, 4)
                for t in range(PAIRS):
                    if t + 5 < PAIRS:
                        sub(b, t + 5)
                    if t % 2 == 0:
                        g = t // 2 + 2
                        if g < GROUPS:
                            no_edge(b + 1, g)
                        elif not (isinstance(b, int) and b == BLOCKS_A - 2):
                            no_edge(b + 2, g - GROUPS)
                    if t + 2 < PAIRS:
                        keep_max(b + 1, t + 2)
                row_max(b + 1)
                take(b)

            with dve.Fori(0, BLOCKS_A - 2) as b:
                step_a(b)
            step_a(BLOCKS_A - 2)
            for t in range(PAIRS):
                sub(BLOCKS_A - 1, t)
            take(BLOCKS_A - 1)
            dve.wait_ge(num_taken, BLOCKS_A)

            PRE = 6

            def choose(l):
                U = U_of[l]
                own = Tally(pre_step, l * PRE)
                dve.wait_ge(wh_taken, 2 * (l + 1) * BLOCKS_G)
                own.inc(dve.tensor_reduce(dmin, U[:, :, D], AX.X, ALU.min))
                own.wait(dve)
                dve.tensor_reduce(dmax, U[:, :, D], AX.X, ALU.max).then_inc(dmm_ready, 1)
                dve.wait_ge(hT_ready, 2 * (l + 2) * BLOCKS_G)
                dve.tensor_reduce(hsum, hs_part[:, :], AX.X, ALU.add).then_inc(hsum_ready, 1)
                dve.wait_ge(dT_ready, l + 1)
                dve.tensor_reduce(k0s[0:1, :], ps[0:1, 6 * 512:6 * 512 + P], AX.X, ALU.max).then_inc(k0_ready, 1)
                own.inc(dve.tensor_reduce(k1s[0:1, :], ps[0:1, 6 * 512 + P:6 * 512 + 2 * P], AX.X, ALU.min))
                dve.wait_ge(k0_ready, l + 1)
                own.wait(dve)
                own.inc(dve.tensor_tensor(k1s[0:1, :], k0s[0:1, :], k1s[0:1, :], ALU.subtract))
                own.wait(dve)
                dve.tensor_scalar(path[:, :], k1s[0:1, :], SPREAD, None, ALU.is_gt).then_inc(path_ready, 1)
                dve.wait_ge(kb_ready, l + 1)
                own.inc(dve.tensor_copy(K0, bank(7, 1)))
                own.wait(dve)
                own.inc(dve.tensor_scalar(K08, K0, 1.0 - SLOPE, None, ALU.mult))
                own.wait(dve)
                dve.tensor_scalar(nK0, K0, -1.0, None, ALU.mult).then_inc(k_ready, 1)
                dve.wait_ge(sumb_ready, l + 1)
                own.inc(dve.tensor_copy(sum_b[:, :], bank(7, D)))
                dve.wait_ge(s_taken, 2 * (l + 1) * BLOCKS_G)
                own.wait(dve)
                assert own.n == PRE, own.n

            def factored(l):
                U, R = U_of[l], R_of[l]
                for s, n in ((x_ones, 2), (x_step, X_STEPS[l] * BLOCKS_X), (x_masked, BLOCKS_X),
                             (x_part, BLOCKS_X), (x_mc, BLOCKS_X), (x_sub, BLOCKS_X)):
                    dve.sem_inc(s, n)
                if l == ELU_LAYER:
                    dve.sem_inc(x_neg, BLOCKS_X)

                def row_factor(q):
                    rs = R[:, ds(q * WG, WG)]
                    dve.tensor_scalar(rs, rs, K0, 0.0, ALU.add, ALU.max).then_inc(rlin_ready, 1)

                row_factor(0)
                dve.wait_ge(bq_ready, 2 * (l + 1))
                for c in range(CHUNKS):
                    cs = slice(c * CHUNK, (c + 1) * CHUNK)
                    dve.tensor_tensor(U[:, cs, 0:D], U[:, cs, 0:D],
                                      B[:, cs].unsqueeze(2).to_broadcast([P, CHUNK, D]),
                                      ALU.mult).then_inc(u_ready, 1)
                    dve.tensor_copy(U[:, cs, D], B[:, cs]).then_inc(u_ready, 1)

                def weights(q, j):
                    n = (l * BLOCKS_G + q) * TILES + j
                    s = j // SAVE
                    if j % SAVE == 0:
                        dve.wait_ge(mask_in[s % 2], 16 * ((l * BLOCKS_G + q) * 2 + s // 2 + 1))
                    dve.wait_ge(z_ready, n + 1)
                    dve.wait_ge(p_free, n + 1)
                    two = "p (h w) -> p h w"
                    dve.scalar_tensor_tensor(out=pring[:, j % RING, :].rearrange(two, h=2),
                                             in0=zring[:, j % RING, :].rearrange(two, h=2), scalar=1.0,
                                             in1=maskb[:, s % 2, :, j % SAVE, :], op0=ALU.add, op1=ALU.mult
                                             ).then_inc(p_made, 1)

                FIN = 6

                def finish1(q):
                    fin = Tally(fin_step, (l * BLOCKS_G + q) * FIN)
                    dve.wait_ge(p_free, (l * BLOCKS_G + q + 1) * TILES + RING)
                    empty, den, inv = (den_r[:, i * SUB_G:(i + 1) * SUB_G] for i in range(3))
                    accs = [ps[:, ds((q % 2) * 1024 + i * 512, 3 * E)].rearrange("p (c k) -> p c k", k=E)
                            for i in range(2)]
                    for i in range(2):
                        fin.inc(dve.tensor_scalar(empty[:, 3 * i:3 * i + 3], accs[i][:, :, D], 0.0, None,
                                                  ALU.is_equal))
                    fin.wait(dve)
                    for i in range(2):
                        fin.inc(dve.scalar_tensor_tensor(out=den[:, 3 * i:3 * i + 3], in0=empty[:, 3 * i:3 * i + 3],
                                                         scalar=float(N), in1=accs[i][:, :, D], op0=ALU.mult,
                                                         op1=ALU.add))
                    fin.wait(dve)
                    fin.inc(dve.reciprocal(inv, den))
                    for c in range(SUB_G):
                        mm = dve.scalar_tensor_tensor(out=o_buf[:, c * D:(c + 1) * D], in0=sum_b[:, :],
                                                      scalar=empty[:, c:c + 1], in1=accs[c // 3][:, c % 3, 0:D],
                                                      op0=ALU.mult, op1=ALU.add)
                    mm.then_inc(acc_free, 1)
                    dve.wait_ge(acc_free, l * BLOCKS_G + q + 1 + 2)
                    fin.wait(dve)
                    six = "p (c d) -> p c d"
                    fin.inc(dve.tensor_tensor(o_buf.rearrange(six, d=D), o_buf.rearrange(six, d=D),
                                              inv.unsqueeze(2).to_broadcast([P, SUB_G, D]), ALU.mult))
                    fin.wait(dve)
                    assert fin.n == FIN
                    if l == ELU_LAYER:
                        dve.tensor_scalar(neg_o, o_buf, 0.0, None, ALU.min).then_inc(neg_ready, 1)

                def finish2(q):
                    if l == ELU_LAYER:
                        dve.wait_ge(expo_ready, q + 1)
                        dve.tensor_scalar(exp_o, exp_o, -1.0, None, ALU.add).then_inc(elu_step, 1)
                        dve.wait_ge(elu_step, 2 * q + 1)
                        dve.scalar_tensor_tensor(out=o_buf, in0=o_buf, scalar=0.0, in1=exp_o, op0=ALU.max,
                                                 op1=ALU.add).then_inc(elu_step, 1)
                        dve.wait_ge(elu_step, 2 * q + 2)
                    xs = X[:, ds(q * SUB_G, SUB_G), :]
                    dve.tensor_tensor(xs, xs, o_buf.rearrange("p (c d) -> p c d", d=D), ALU.add).then_inc(x_done, 1)

                def block_g(q, last, more):
                    for j in range(TILES):
                        if last is not None:
                            if j == 6:
                                finish1(last)
                            if j == 11:
                                finish2(last)
                            if l + 1 < LAYERS:
                                if j == 14:
                                    hold(dve, x_done, l * BLOCKS_G + last + 1)
                                    moments(l + 2, last, 0)
                                if j == 21:
                                    normalize(l + 2, last, 0, h_blk[:, :])
                        if j == 30 and more:
                            row_factor(q + 1)
                        weights(q, j)

                block_g(0, None, True)
                with dve.Fori(1, BLOCKS_G - 1) as q:
                    block_g(q, q - 1, True)
                block_g(BLOCKS_G - 1, BLOCKS_G - 2, False)
                finish1(BLOCKS_G - 1)
                finish2(BLOCKS_G - 1)
                if l + 1 < LAYERS:
                    dve.wait_ge(x_done, (l + 1) * BLOCKS_G)
                    moments(l + 2, BLOCKS_G - 1, 0)
                    normalize(l + 2, BLOCKS_G - 1, 0, h_blk[:, :])

            def general(l):
                U, R = U_of[l], R_of[l]
                M = spare_of[l]
                for s, n in ((rlin_ready, BLOCKS_G), (u_ready, 2 * CHUNKS), (p_made, BLOCKS_G * TILES),
                             (acc_free, BLOCKS_G), (fin_step, 6 * BLOCKS_G), (x_done, BLOCKS_G - 1)):
                    dve.sem_inc(s, n)
                if l == ELU_LAYER:
                    dve.sem_inc(neg_ready, BLOCKS_G)
                    dve.sem_inc(elu_step, 2 * BLOCKS_G)
                dve.tensor_copy(B[:, :], U[:, :, D]).then_inc(x_ones, 1)
                dve.wait_ge(x_ones, 2 * l + 1)
                dve.memset(U[:, :, D:E], 1.0).then_inc(x_ones, 1)
                Sx = h_all.rearrange("p (t w) -> p t w", w=QUERIES)
                with dve.Fori(0, BLOCKS_X) as b:
                    n = l * BLOCKS_X + b
                    own = Tally(x_step, sum(X_STEPS[:l]) * BLOCKS_X + b * X_STEPS[l])
                    rows = R[:, ds(b * QUERIES, QUERIES)].unsqueeze(1).to_broadcast([P, TILES, QUERIES])
                    own.inc(dve.tensor_tensor(Sx, B[:, :].unsqueeze(2).to_broadcast([P, TILES, QUERIES]), rows,
                                              ALU.add))
                    own.wait(dve)
                    own.inc(dve.scalar_tensor_tensor(out=Sx, in0=Sx, scalar=SLOPE, in1=Sx, op0=ALU.mult, op1=ALU.max))
                    dve.wait_ge(x_mask_in, 16 * SAVES * (n + 1))
                    dve.tensor_scalar(M.rearrange("p (t w) -> p t w", w=QUERIES), maskx[:, :, :], -0.5, -2.0 * MASKED,
                                      ALU.add, ALU.mult).then_inc(x_masked, 1)
                    dve.wait_ge(x_masked, n + 2)
                    own.wait(dve)
                    own.inc(dve.tensor_tensor(h_all, h_all, M, ALU.min))
                    own.wait(dve)
                    dve.tensor_reduce(part_max[:, 0:P], Sx.rearrange("p t w -> p w t"), AX.X, ALU.max
                                      ).then_inc(x_part, 1)
                    dve.wait_ge(x_mT, n + 1)
                    dve.tensor_reduce(max_c[:, 0:1], bank(7, P), AX.X, ALU.max).then_inc(x_mc, 1)
                    dve.wait_ge(x_mb, n + 1)
                    dve.tensor_tensor(Sx, Sx, bank(7, P).unsqueeze(1).to_broadcast([P, TILES, QUERIES]),
                                      ALU.subtract).then_inc(x_sub, 1)
                    dve.wait_ge(x_av, n + 1)
                    own.inc(dve.reciprocal(den_r[:, 0:1], bank(6, E)[:, D:E]))
                    own.wait(dve)
                    own.inc(dve.tensor_scalar(o_buf[:, 0:D], bank(6, D), den_r[:, 0:1], None, ALU.mult))
                    own.wait(dve)
                    if l == ELU_LAYER:
                        dve.tensor_scalar(neg_o[:, 0:D], o_buf[:, 0:D], 0.0, None, ALU.min).then_inc(x_neg, 1)
                        dve.wait_ge(x_eo, b + 1)
                        own.inc(dve.tensor_scalar(exp_o[:, 0:D], exp_o[:, 0:D], -1.0, None, ALU.add))
                        own.wait(dve)
                        own.inc(dve.scalar_tensor_tensor(out=o_buf[:, 0:D], in0=o_buf[:, 0:D], scalar=0.0,
                                                         in1=exp_o[:, 0:D], op0=ALU.max, op1=ALU.add))
                        own.wait(dve)
                    xs = X[:, ds(b, 1), :].rearrange("p o d -> p (o d)")
                    own.inc(dve.tensor_tensor(xs, xs, o_buf[:, 0:D], ALU.add))
                    own.wait(dve)
                    assert own.n == X_STEPS[l], own.n
                dve.sem_inc(x_done, 1)
                if l + 1 < LAYERS:
                    all_blocks(l + 2)

            all_blocks(1)
            for l in range(LAYERS):
                choose(l)
                either_path(dve, l, general, factored)


def kernel(x, adj, L0_gnn_input, L0_gnn_weight, L1_gnn_W, L1_gnn_a, L2_gnn_W, L2_gnn_a, L3_gnn_W, L3_gnn_a):
    import numpy as np
    import concourse.bacc as bacc
    from concourse.bass_utils import run_bass_kernel_spmd

    def rows(a):
        return np.ascontiguousarray(np.asarray(a).reshape(TILES, P, D).transpose(1, 0, 2))

    adj_t = np.ascontiguousarray(
        np.asarray(adj).reshape(BLOCKS_A, WA, GROUPS, GROUP, P).transpose(0, 2, 4, 3, 1)
    ).reshape(BLOCKS_A, GROUPS, P, GROUP * WA)
    arrays = {
        "x": rows(x), "adj": adj_t, "values": rows(L0_gnn_input),
        "keys": np.ascontiguousarray(np.asarray(L0_gnn_input).T),
        "w0": np.asarray(L0_gnn_weight), "w1": np.asarray(L1_gnn_W), "w2": np.asarray(L2_gnn_W),
        "w3": np.asarray(L3_gnn_W),
        "a1": np.asarray(L1_gnn_a).reshape(1, 2 * D), "a2": np.asarray(L2_gnn_a).reshape(1, 2 * D),
        "a3": np.asarray(L3_gnn_a).reshape(1, 2 * D),
    }
    nc = bacc.Bacc("TRN2", target_bir_lowering=False, num_devices=1, dynamic_dma_scratch_size=256)
    t = {n: nc.dram_tensor(n + "_dram", a.shape, mybir.dt.from_np(a.dtype), kind="ExternalInput").ap()
         for n, a in arrays.items()}
    out = nc.dram_tensor("out_dram", (P, TILES, D), F32, kind="ExternalOutput").ap()
    mask_scr = nc.dram_tensor("mask_scr", (BLOCKS_A, SAVES, P, SAVE * WA), U8, kind="Internal").ap()
    g_scr = nc.dram_tensor("g_scr", (BLOCKS_A, P, 2 * WA), F32, kind="Internal").ap()
    program(nc, t["x"], t["adj"], t["values"], t["keys"], [t[f"w{i}"] for i in range(4)],
            [t[f"a{i}"] for i in range(1, 4)], mask_scr, g_scr, out)
    r = run_bass_kernel_spmd(nc, [{n + "_dram": a for n, a in arrays.items()}], core_ids=[0])
    return r.results[0]["out_dram"].transpose(1, 0, 2).reshape(N, D)
```

```python
from contextlib import ExitStack

import concourse.bass as bass
from concourse import mybir

F32 = mybir.dt.float32
F32R = mybir.dt.float32r
BF16 = mybir.dt.bfloat16
I32 = mybir.dt.int32
U8 = mybir.dt.uint8
ALU = mybir.AluOpType
ACT = mybir.ActivationFunctionType
AX = mybir.AxisListType

P = 128
N = 6144
D = 128
TILES = N // P
LAYERS = 3
TEMPERATURE = 0.07
SLOPE = 0.2
EPS = 1e-5
MASKED = -2.0 ** 100

WA = 384
BLOCKS_A = N // WA
SUB_A = WA // P
PAIRS = TILES // 2
GROUP = 4
GROUPS = TILES // GROUP
SAVE = 12
SAVES = TILES // SAVE

WG = 2 * WA
BLOCKS_G = N // WG
SUB_G = WG // P
RING = 6
CREDIT = 13
E = D + 1
CHUNK = 12
CHUNKS = TILES // CHUNK
CONSTS = 5
X_LOADS = 4
STAGED = 8
LEAD = 3
SLOTS = 4
SPREAD = 60.0
X_STEPS = [6, 8, 6]
QUERIES = 128
BLOCKS_X = N // QUERIES
ELU_LAYER = 1


class Tally:

    def __init__(self, sem, base):
        self.sem, self.base, self.n = sem, base, 0

    def inc(self, instruction):
        instruction.then_inc(self.sem, 1)
        self.n += 1

    def wait(self, engine):
        engine.wait_ge(self.sem, self.base + self.n)


def ds(start, size):
    return bass.ds(start, size)


def program(nc, x_in, adj_in_d, inp_nat, inp_t, w_in, a_in, mask_scr, g_scr, out_d):
    ctx = ExitStack()
    with ctx:
        def sb(name, shape, dt):
            return ctx.enter_context(nc.sbuf_tensor(name, shape, dt))

        def sem(name):
            return ctx.enter_context(nc.semaphore(name))

        arena = sb("arena", [P, TILES * WA], F32)
        S = arena[:, :].rearrange("p (t w) -> p t w", w=WA)
        third = [arena[:, i * N:(i + 1) * N] for i in range(3)]
        h_all = third[0]
        pring = arena[:, 0:RING * WG].rearrange("p (s w) -> p s w", w=WG)
        R_of = [third[2], third[1], third[2]]
        spare_of = [third[1], third[2], third[1]]
        key_hi = sb("key_hi", [P, N], F32R)
        key_lo = sb("key_lo", [P, N], F32R)
        maskb = key_hi[:, 0:2 * 2 * SAVE * WA // 4].bitcast(U8).rearrange(
            "p (s h k w) -> p s h k w", s=2, h=2, k=SAVE)
        maskx = key_lo[:, 0:TILES * QUERIES // 4].bitcast(U8).rearrange("p (t w) -> p t w", w=QUERIES)
        U0 = sb("U0", [P, TILES, E], F32)
        X = sb("X", [P, TILES, D], F32)
        ADJ, NOT, SAV = 3 * GROUP * WA, 3 * GROUP * WA // 2, 2 * SAVE * WA // 4
        stage = sb("stage", [P, ADJ + NOT + SAV], I32)
        adjb = stage[:, 0:ADJ].rearrange("p (s w) -> p s w", s=3)
        notb = stage[:, ADJ:ADJ + NOT].bitcast(BF16).rearrange("p (s w) -> p s w", s=3)
        saveb = stage[:, ADJ + NOT:ADJ + NOT + SAV].bitcast(U8).rearrange("p (s w) -> p s w", s=2)
        stagef = stage[:, :].bitcast(F32)
        U1 = stagef[:, 0:TILES * E].rearrange("p (t k) -> p t k", k=E)
        U_of = [U0, U1, U0]
        hT_blk, neg_o, exp_o = (stagef[:, TILES * E + i * WG:TILES * E + (i + 1) * WG] for i in range(3))
        Wraw = stagef[:, ADJ:ADJ + 4 * D].rearrange("p (l f) -> p l f", l=4)
        a_rows = stagef[:, ADJ + NOT:ADJ + NOT + LAYERS * 2 * D].rearrange("p (l f) -> p l f", l=LAYERS)
        w_dot = stagef[:, ADJ + NOT + LAYERS * 2 * D:ADJ + NOT + (LAYERS * 2 + 1) * D]
        G = sb("G", [P, 4 * WA], F32R)
        run_max = sb("run_max", [P, 2, WA], F32)
        o_buf = run_max[:, :, :].rearrange("p a w -> p (a w)")
        part_max = sb("part_max", [P, WA], F32)
        h_blk = sb("h_blk", [P, WG], F32)
        max_c = sb("max_c", [P, SUB_A], F32)
        identF = sb("identF", [P, P], F32)
        negI = sb("negI", [P, P], BF16)
        WX = sb("WX", [P, LAYERS, E], F32)
        va1 = sb("va1", [P, LAYERS], F32)
        sum_b = sb("sum_b", [P, D], F32)
        stats = sb("stats", [P, SUB_G, 6], F32)
        mv = sb("mv", [P, SLOTS, SUB_G, 2], F32)
        var = sb("var", [P, SLOTS, SUB_G], F32)
        rstd = sb("rstd", [P, SLOTS, SUB_G], F32)
        shift = sb("shift", [P, SLOTS, SUB_G], F32)
        B = sb("B", [P, TILES], F32)
        T = sb("T", [P, TILES], F32)
        hs_part = sb("hs_part", [P, N // WA], F32)
        st = sb("st", [P, 16], F32)
        den_r = sb("den_r", [P, 3 * SUB_G], F32)
        path = sb("path", [1, 1], I32)
        one_row = sb("one_row", [1, P], F32)
        K0, T_bias, B_bias, dmax, dmin, hsum, k0s, k1s, warm = (st[:, i:i + 1] for i in range(9))
        ps = ctx.enter_context(nc.psum_tensor("ps", [P, 8 * 512], F32))

        def bank(i, n):
            return ps[:, i * 512:i * 512 + n]

        x_in_s = [sem(f"x_in{i}") for i in range(X_LOADS)]
        key_in, val_in, w_in_s, consts = (sem(n) for n in ("key_in", "val_in", "w_in", "consts"))
        dve_pro, key_split, wx_ready = sem("dve_pro"), sem("key_split"), sem("wx_ready")
        stat_ready, aggr_ready, var_ready, std_ready, shift_ready, rc_ready, h_ready, tr_ready, hT_ready = (
            sem(n) for n in ("stat_ready", "aggr_ready", "var_ready", "std_ready", "shift_ready", "rc_ready", "h_ready",
                             "tr_ready", "hT_ready"))
        g_ready, g_half, g_made, g_in = sem("g_ready"), sem("g_half"), sem("g_made"), sem("g_in")
        g_staged = sem("g_staged")
        g_stored = [sem(f"g_stored{i}") for i in range(2)]
        adj_in = [sem(f"adj_in{i}") for i in range(3)]
        not_made, save_made = sem("not_made"), sem("save_made")
        saved = [sem(f"saved{i}") for i in range(2)]
        scores_ready, evac_done, max_done, part_ready, mT_ready, mc_ready, mb_ready = (
            sem(n) for n in ("scores_ready", "evac_done", "max_done", "part_ready", "mT_ready", "mc_ready",
                             "mb_ready"))
        sub_done, exp_done, av_done, rden_ready, num_taken = (
            sem(n) for n in ("sub_done", "exp_done", "av_done", "rden_ready", "num_taken"))
        pre_step, wh_ready, wh_taken, s_ready, s_taken = (
            sem(n) for n in ("pre_step", "wh_ready", "wh_taken", "s_ready", "s_taken"))
        dmm_ready, dT_ready, k0_ready, kb_ready, k_ready, path_ready, hsum_ready, sumb_ready = (
            sem(n) for n in ("dmm_ready", "dT_ready", "k0_ready", "kb_ready", "k_ready", "path_ready",
                             "hsum_ready", "sumb_ready"))
        mask_in = [sem(f"mask_in{i}") for i in range(2)]
        bt_ready, rlin_ready, r_ready, u_ready, p_made, p_free, acc_free, fin_step, neg_ready, expo_ready = (
            sem(n) for n in ("bt_ready", "rlin_ready", "r_ready", "u_ready", "p_made", "p_free",
                             "acc_free", "fin_step", "neg_ready", "expo_ready"))
        x_mask_in, x_ones, x_step, x_masked, x_part, x_mT, x_mc, x_mb, x_sub, x_exp, x_av, x_neg, x_eo = (
            sem(n) for n in ("x_mask_in", "x_ones", "x_step", "x_masked", "x_part", "x_mT", "x_mc", "x_mb",
                             "x_sub", "x_exp", "x_av", "x_neg", "x_eo"))
        x_done, elu_step = sem("x_done"), sem("elu_step")
        out_done, idle = sem("out_done"), sem("idle")

        block = ctx.enter_context(nc.Block())

        def hold(engine, semaphore, count):
            engine.wait_ge(semaphore, count)
            engine.sem_inc(idle, 1)

        def g_slot(b):
            if b >= STAGED:
                return key_lo[:, (b - STAGED) * 2 * WA:(b - STAGED + 1) * 2 * WA]
            return G[:, (b % 2) * 2 * WA:(b % 2 + 1) * 2 * WA]

        def turn(k, q):
            return k * BLOCKS_G + (q if k else BLOCKS_G - 1 - q)

        def either_path(engine, l, general, factored):
            engine.wait_ge(path_ready, l + 1)
            choice = engine.value_load(path[0:1, 0:1], min_val=0, max_val=1)
            with engine.If(choice == 1):
                general(l)
            with engine.Else():
                factored(l)

        @block.sync
        def _(sp):
            for i in range(4):
                sp.dma_start(Wraw[:, i, :], w_in[i]).then_inc(w_in_s, 16)
            for i in range(LAYERS):
                sp.dma_start(a_rows[:, i, :], a_in[i].to_broadcast([P, 2 * D])).then_inc(w_in_s, 16)
            for i in range(X_LOADS):
                rows = slice(TILES - (i + 1) * TILES // X_LOADS, TILES - i * TILES // X_LOADS)
                sp.dma_start(X[:, rows, :], x_in[:, rows, :]).then_inc(x_in_s[i], 16)
            sp.dma_start(third[2], inp_t).then_inc(key_in, 16)

            def load_adj(b, g):
                m = b * GROUPS + g
                if not isinstance(m, int) or m >= 3:
                    sp.wait_ge(not_made, m - 2)
                sp.dma_start(adjb[:, g % 3, :], adj_in_d[ds(b, 1), g].rearrange("o p w -> p (o w)")
                             ).then_inc(adj_in[g % 3], 16)

            def store_mask(b, s):
                sp.wait_ge(save_made, b * GROUPS + 3 * s + 3)
                sp.dma_start(mask_scr[ds(b, 1), s].rearrange("o p w -> p (o w)"), saveb[:, s % 2, :]
                             ).then_inc(saved[s % 2], 16)

            def load_g(b):
                sp.dma_start(G[:, ds((b % 2) * 2 * WA, 2 * WA)].bitcast(F32),
                             g_scr[ds(b, 1)].rearrange("o p w -> p (o w)")).then_inc(g_in, 16)

            for g in range(3):
                load_adj(0, g)
            for b in range(BLOCKS_A - 1, 1, -1):
                sp.wait_ge(g_made, BLOCKS_A - b)
                sp.dma_start(g_scr[b], g_slot(b).bitcast(F32)
                             ).then_inc(g_staged if b >= STAGED else g_stored[b % 2], 16)
            sp.dma_start(U0[:, :, 0:D], inp_nat).then_inc(val_in, 16)
            sp.wait_ge(g_staged, 16 * (BLOCKS_A - STAGED))
            for s in g_stored:
                sp.wait_ge(s, 16 * (STAGED // 2 - 1))
            sp.wait_ge(g_made, BLOCKS_A)
            sp.sem_inc(g_in, 2 * 16)

            def adj_block(b, first):
                for g in range(GROUPS):
                    if not (first and g < 3):
                        load_adj(b, g)
                    if g == 2 and not first:
                        store_mask(b - 1, 3)
                    if g in (5, 8, 11):
                        store_mask(b, (g - 5) // 3)
                    if g == 5 and not (isinstance(b, int) and b in (0, BLOCKS_A - 1)):
                        sp.wait_ge(scores_ready, b * PAIRS + 1)
                        load_g(b + 1)

            adj_block(0, True)
            with sp.Fori(1, BLOCKS_A - 1) as b:
                adj_block(b, False)
            adj_block(BLOCKS_A - 1, False)
            store_mask(BLOCKS_A - 1, 3)
            for s in saved:
                sp.wait_ge(s, 16 * BLOCKS_A * SAVES // 2)
            sp.wait_ge(not_made, BLOCKS_A * GROUPS)

            def load_mask(l, q, s):
                hold(sp, p_made, ((l * BLOCKS_G + q) * SAVES + s) * SAVE + CREDIT - SAVE)
                sp.dma_start(
                    maskb[:, s % 2].rearrange("p h k w -> p h (k w)"),
                    mask_scr.rearrange("(q h) s p w -> q s p h w", h=2)[ds(q, 1), s].rearrange(
                        "o p h w -> p (o h) w")).then_inc(mask_in[s % 2], 16)

            def factored(l):
                sp.sem_inc(x_mask_in, 16 * BLOCKS_X * SAVES)
                with sp.Fori(0, BLOCKS_G - 1) as q:
                    load_mask(l, q, 2)
                    load_mask(l, q, 3)
                    load_mask(l, q + 1, 0)
                    load_mask(l, q + 1, 1)
                load_mask(l, BLOCKS_G - 1, 2)
                load_mask(l, BLOCKS_G - 1, 3)

            def general(l):
                for s in mask_in:
                    sp.wait_ge(s, 16 * (l * BLOCKS_G * SAVES // 2 + 1))
                    sp.sem_inc(s, 16 * (BLOCKS_G * SAVES // 2 - 1))
                with sp.Fori(0, BLOCKS_A) as b:
                    for c in range(SUB_A):
                        hold(sp, x_masked, l * BLOCKS_X + b * SUB_A + c + 1)
                        for s in range(SAVES):
                            src = mask_scr[ds(b, 1), s].rearrange("o p (k w) -> p (o k) w", w=WA)
                            dma = sp.dma_start(maskx[:, s * SAVE:(s + 1) * SAVE, :],
                                               src[:, :, c * QUERIES:(c + 1) * QUERIES])
                            dma.then_inc(x_mask_in, 16)

            sp.wait_ge(scores_ready, BLOCKS_A * PAIRS)
            for l in range(LAYERS):
                load_mask(l, 0, 0)
                load_mask(l, 0, 1)
                either_path(sp, l, general, factored)
            early = (BLOCKS_G - 1) * SUB_G
            sp.wait_ge(x_done, LAYERS * BLOCKS_G - 1)
            sp.dma_start(out_d[:, 0:early, :], X[:, 0:early, :]).then_inc(out_done, 16)
            sp.wait_ge(x_done, LAYERS * BLOCKS_G)
            sp.dma_start(out_d[:, early:TILES, :], X[:, early:TILES, :]).then_inc(out_done, 16)
            sp.wait_ge(out_done, 32)

        @block.gpsimd
        def _(pool):
            pool.memset(identF[:, :], 0.0).then_inc(consts, 1)
            pool.memset(negI[:, :], 0.0).then_inc(consts, 1)
            pool.wait_ge(consts, 2)
            pool.affine_select(out=identF[:, :], in_=identF[:, :], compare_op=ALU.not_equal, fill=1.0,
                               base=0, pattern=[[-1, P]], channel_multiplier=1).then_inc(consts, 1)
            pool.affine_select(out=negI[:, :], in_=negI[:, :], compare_op=ALU.not_equal, fill=MASKED,
                               base=0, pattern=[[-1, P]], channel_multiplier=1).then_inc(consts, 1)
            pool.memset(one_row[:, :], 1.0).then_inc(consts, 1)

        @block.tensor
        def _(pe):
            pe.wait_ge(consts, CONSTS)

            def transposes(k, q, h):
                n = turn(k, q)
                pe.wait_ge(h_ready, n + 1)
                for i in range(2):
                    for c in range(3 * i, 3 * i + 3):
                        mm = pe.transpose(bank(4 + i, 512)[:, (c % 3) * P:(c % 3 + 1) * P],
                                          h[:, c * D:(c + 1) * D], identF[:, :])
                    mm.then_inc(tr_ready, 1)

            def project(l, q, hT, banks=4):
                for i in range(2):
                    pe.wait_ge(hT_ready, 2 * ((l + 1) * BLOCKS_G + q) + i + 1)
                    half = hT[:, i * WA:(i + 1) * WA]
                    for c in range(3):
                        mm = pe.matmul(bank(6 + i, 512)[:, c * E:(c + 1) * E], half[:, c * P:(c + 1) * P],
                                       WX[:, l, :], start=True, stop=True)
                    mm.then_inc(wh_ready, 1)
                    pe.matmul(bank(banks + i, WA), va1[:, l:l + 1].to_broadcast([P, P]), half,
                              start=True, stop=True).then_inc(s_ready, 1)

            def g_rows(q):
                for b in (2 * q + 1, 2 * q):
                    i = BLOCKS_A - 1 - b
                    pe.wait_ge(hT_ready, 2 * turn(0, q) + 2)
                    if i >= 2:
                        pe.wait_ge(g_made, i - 1)
                    pe.matmul(bank(2 + b % 2, WA), Wraw[:, 0, :], third[1][:, b * WA:(b + 1) * WA],
                              start=True, stop=True).then_inc(g_ready, 1)

            for i in range(BLOCKS_G + 1):
                q = BLOCKS_G - 1 - i
                if q >= 0:
                    if i >= 1:
                        pe.wait_ge(hT_ready, 2 * i)
                    transposes(0, q, h_all[:, q * WG:(q + 1) * WG])
                if i == 0:
                    pe.wait_ge(w_in_s, 16 * (4 + LAYERS))
                else:
                    g_rows(q + 1)

            def gen(b, t):
                n = b * PAIRS + t
                if t == 0:
                    pe.wait_ge(g_in, 16 * (b + 1))
                if not isinstance(n, int) or n >= 3:
                    pe.wait_ge(evac_done, n - 2)
                if t % 2 == 0:
                    pe.wait_ge(not_made, b * GROUPS + t // 2 + 1)
                g_hi = G[:, ds((b % 2) * 2 * WA, WA)]
                g_lo = G[:, ds((b % 2) * 2 * WA + WA, WA)]
                for q in range(2):
                    o = bank(2 * (t % 3) + q, WA)
                    c = slice((2 * t + q) * P, (2 * t + q + 1) * P)
                    m = (2 * (t % 2) + q) * WA
                    pe.matmul(o, key_hi[:, c], g_hi, start=True, stop=False)
                    pe.matmul(o, key_hi[:, c], g_lo, start=False, stop=False)
                    pe.matmul(o, key_lo[:, c], g_hi, start=False, stop=False)
                    mm = pe.matmul(o, negI[:, :], notb[:, (t // 2) % 3, m:m + WA], start=False, stop=True)
                mm.then_inc(scores_ready, 1)

            def row_max_t(b):
                pe.wait_ge(part_ready, b + 1)
                for c in range(SUB_A):
                    mm = pe.transpose(bank(7, WA)[:, c * P:(c + 1) * P], part_max[:, c * P:(c + 1) * P],
                                      identF[:, :])
                mm.then_inc(mT_ready, 1)

            def row_max_b(b):
                pe.wait_ge(mc_ready, b + 1)
                for c in range(SUB_A):
                    mm = pe.matmul(bank(7, WA)[:, c * P:(c + 1) * P], max_c[:, c:c + 1].to_broadcast([P, P]),
                                   identF[:, :], start=True, stop=True)
                mm.then_inc(mb_ready, 1)

            def av(b, t, halves=(0, 1)):
                pe.wait_ge(exp_done, b * PAIRS + t + 1)
                if t == 0 and not (isinstance(b, int) and b == 0):
                    pe.wait_ge(num_taken, b)
                for q in halves:
                    for c in range(SUB_A):
                        mm = pe.matmul(bank(6, 512)[:, c * E:(c + 1) * E], S[:, 2 * t + q, c * P:(c + 1) * P],
                                       U0[:, 2 * t + q, :], start=(t == 0 and q == 0 and c == 0),
                                       stop=(t == PAIRS - 1 and q == 1), skip_group_check=True)
                if 1 in halves:
                    mm.then_inc(av_done, 1)

            def turn_block(l, q):
                if q >= 1:
                    pe.wait_ge(hT_ready, 2 * ((l + 1) * BLOCKS_G + q))
                transposes(l + 1, q, h_all[:, q * WG:(q + 1) * WG])

            pe.wait_ge(key_split, 2)
            pe.wait_ge(g_made, BLOCKS_A)
            for t in range(PAIRS):
                gen(0, t)
            row_max_t(0)
            row_max_b(0)
            pe.wait_ge(val_in, 16)
            pe.wait_ge(wx_ready, 1)

            def step_a(b):
                gen(b + 1, 0)
                gen(b + 1, 1)
                for t in range(PAIRS - 1):
                    av(b, t)
                    if t + 2 < PAIRS:
                        gen(b + 1, t + 2)
                row_max_t(b + 1)
                av(b, PAIRS - 1, (0,))
                row_max_b(b + 1)
                av(b, PAIRS - 1, (1,))

            with pe.Fori(0, BLOCKS_A - 2) as b:
                step_a(b)
            step_a(BLOCKS_A - 2)
            for t in range(PAIRS):
                av(BLOCKS_A - 1, t)
                if t in (PAIRS - 6, PAIRS - 3, PAIRS - 1):
                    turn_block(0, (t - PAIRS + 6 + 1) // 3)

            def project_all(l, hT):
                for q in range(BLOCKS_G):
                    if q >= 1:
                        pe.wait_ge(wh_taken, 2 * (l * BLOCKS_G + q))
                        pe.wait_ge(s_taken, 2 * (l * BLOCKS_G + q))
                    project(l, q, hT[:, q * WG:(q + 1) * WG], 2)
                    if q + LEAD < BLOCKS_G:
                        turn_block(l, q + LEAD)

            def choose(l):
                pe.wait_ge(dmm_ready, l + 1)
                pe.transpose(ps[0:1, 6 * 512:6 * 512 + P], dmax, identF[:, :])
                pe.transpose(ps[0:1, 6 * 512 + P:6 * 512 + 2 * P], dmin, identF[:, :]).then_inc(dT_ready, 1)
                pe.wait_ge(k0_ready, l + 1)
                pe.matmul(bank(7, 1), one_row[:, :], k0s[0:1, :], start=True, stop=True).then_inc(kb_ready, 1)
                pe.wait_ge(hsum_ready, l + 1)
                pe.wait_ge(k_ready, l + 1)
                pe.matmul(bank(7, D), hsum.to_broadcast([P, P]), WX[:, l, 0:D],
                          start=True, stop=True).then_inc(sumb_ready, 1)

            def factored(l):
                for s in (x_mT, x_mb, x_av):
                    pe.sem_inc(s, BLOCKS_X)
                pe.wait_ge(sumb_ready, l + 1)

                def sums(q, s, j):
                    pe.wait_ge(p_made, (l * BLOCKS_G + q) * TILES + j + 1 + CREDIT)
                    for c in range(SUB_G):
                        mm = pe.matmul(bank(2 * s + c // 3, 512)[:, (c % 3) * E:(c % 3 + 1) * E],
                                       pring[:, j % RING, c * P:(c + 1) * P], U_of[l][:, j, :],
                                       start=(j == 0 and c % 3 == 0), stop=(j == TILES - 1),
                                       skip_group_check=True)
                    mm.then_inc(p_free, 1)

                def block_g(q, s, last):
                    pe.wait_ge(acc_free, l * BLOCKS_G + q + 1)
                    for j in range(TILES):
                        if isinstance(q, int) and q == 0 and j % CHUNK == 0:
                            pe.wait_ge(u_ready, 2 * (l * CHUNKS + j // CHUNK + 1))
                        if l + 1 < LAYERS and last is not None:
                            if j == 22:
                                transposes(l + 2, last, h_blk[:, :])
                            if j == 28:
                                project(l + 1, last, hT_blk)
                        sums(q, s, j)

                block_g(0, 0, None)
                block_g(1, 1, 0)
                with pe.Fori(1, BLOCKS_G // 2) as qq:
                    for s in range(2):
                        block_g(qq * 2 + s, s, qq * 2 + s - 1)
                if l + 1 < LAYERS:
                    transposes(l + 2, BLOCKS_G - 1, h_blk[:, :])
                    project(l + 1, BLOCKS_G - 1, hT_blk)

            def general(l):
                pe.sem_inc(p_free, BLOCKS_G * TILES)
                pe.wait_ge(x_ones, 2 * (l + 1))
                pe.wait_ge(sumb_ready, l + 1)
                with pe.Fori(0, BLOCKS_X) as b:
                    n = l * BLOCKS_X + b
                    pe.wait_ge(x_part, n + 1)
                    pe.transpose(bank(7, P), part_max[:, 0:P], identF[:, :]).then_inc(x_mT, 1)
                    pe.wait_ge(x_mc, n + 1)
                    pe.matmul(bank(7, P), max_c[:, 0:1].to_broadcast([P, P]), identF[:, :],
                              start=True, stop=True).then_inc(x_mb, 1)
                    pe.wait_ge(x_exp, n + 1)
                    for j in range(TILES):
                        mm = pe.matmul(bank(6, E), h_all[:, j * QUERIES:(j + 1) * QUERIES], U_of[l][:, j, :],
                                       start=(j == 0), stop=(j == TILES - 1))
                    mm.then_inc(x_av, 1)
                if l + 1 < LAYERS:
                    for q in range(LEAD):
                        turn_block(l + 1, q)
                    project_all(l + 1, spare_of[l + 1])

            pe.wait_ge(num_taken, BLOCKS_A)
            project_all(0, third[1])
            for l in range(LAYERS):
                choose(l)
                either_path(pe, l, general, factored)

        @block.scalar
        def _(act):
            def roots(k, q, slot):
                act.wait_ge(var_ready, turn(k, q) + 1)
                act.activation(rstd[:, slot, :], var[:, slot, :], ACT.Sqrt).then_inc(std_ready, 1)

            def relu_T(k, q, hT):
                for i in range(2):
                    hold(act, tr_ready, 2 * turn(k, q) + i + 1)
                    act.activation(hT[:, i * WA:(i + 1) * WA], bank(4 + i, WA), ACT.Relu,
                                   accum_out=hs_part[:, ds(2 * q + i, 1)]).then_inc(hT_ready, 1)

            def projected(l, q, banks=4):
                for i in range(2):
                    hold(act, wh_ready, 2 * (l * BLOCKS_G + q) + i + 1)
                    act.activation(U_of[l][:, ds(6 * q + 3 * i, 3), :],
                                   bank(6 + i, 3 * E).rearrange("p (c k) -> p c k", k=E), ACT.Copy
                                   ).then_inc(wh_taken, 1)
                    hold(act, s_ready, 2 * (l * BLOCKS_G + q) + i + 1)
                    act.activation(R_of[l][:, ds((2 * q + i) * WA, WA)], bank(banks + i, WA), ACT.Copy
                                   ).then_inc(s_taken, 1)

            def all_blocks(k, hT, l):
                for q in range(BLOCKS_G + LEAD):
                    if q < BLOCKS_G:
                        roots(k, q, q % 2)
                    if 1 <= q <= BLOCKS_G:
                        relu_T(k, q - 1, hT[:, (q - 1) * WG:q * WG])
                    if q >= LEAD:
                        projected(l, q - LEAD, 2)

            def high_g(q):
                for b in (2 * q + 1, 2 * q):
                    i = BLOCKS_A - 1 - b
                    act.wait_ge(g_ready, i + 1)
                    if b < STAGED - 2:
                        act.wait_ge(g_stored[b % 2], 16 * ((STAGED - 1 - b) // 2))
                    act.activation(g_slot(b)[:, 0:WA], bank(2 + b % 2, WA), ACT.Copy).then_inc(g_half, 1)

            for i in range(BLOCKS_G + 3):
                q = BLOCKS_G - 1 - i
                if q >= 0:
                    roots(0, q, i % SLOTS)
                if 0 <= q + 1 < BLOCKS_G:
                    act.wait_ge(shift_ready, i)
                    for c in range(SUB_G):
                        slot = (i - 1) % SLOTS
                        mm = act.activation(h_all[:, (q + 1) * WG + c * D:(q + 1) * WG + (c + 1) * D],
                                            X[:, (q + 1) * SUB_G + c, :], ACT.Identity,
                                            scale=rstd[:, slot, c:c + 1], bias=shift[:, slot, c:c + 1])
                    mm.then_inc(h_ready, 1)
                if 0 <= q + 2 < BLOCKS_G:
                    relu_T(0, q + 2, third[1][:, (q + 2) * WG:(q + 3) * WG])
                if 0 <= q + 3 < BLOCKS_G:
                    high_g(q + 3)

            def evac(b, t):
                n = b * PAIRS + t
                act.wait_ge(max_done, n + 1)
                if not (isinstance(b, int) and b == 0):
                    act.wait_ge(av_done, (b - 1) * PAIRS + t + 1)
                src = ps[:, 2 * (t % 3) * 512:(2 * (t % 3) + 2) * 512].rearrange("p (q w) -> p q w", q=2)
                act.activation(S[:, 2 * t:2 * t + 2, :], src[:, :, 0:WA], ACT.Copy).then_inc(evac_done, 1)

            def save(b, g):
                act.wait_ge(not_made, b * GROUPS + g + 1)
                s = g // 3
                if g % 3 == 0 and not (isinstance(b, int) and b == 0 and s < 2):
                    act.wait_ge(saved[s % 2], 16 * (b * 2 + s // 2))
                act.activation(saveb[:, s % 2, (g % 3) * GROUP * WA:(g % 3 + 1) * GROUP * WA], notb[:, g % 3, :],
                               ACT.Copy, scale=-1.0, bias=1.0).then_inc(save_made, 1)

            def exps(b, t):
                act.wait_ge(sub_done, b * PAIRS + t + 1)
                act.activation(S[:, 2 * t:2 * t + 2, :], S[:, 2 * t:2 * t + 2, :], ACT.Exp,
                               scale=1.0 / TEMPERATURE).then_inc(exp_done, 1)

            for t in range(PAIRS):
                evac(0, t)
                if t % 2 == 0:
                    save(0, t // 2)

            def first_half(b):
                for t in range(3):
                    exps(b, t)
                pairs(b, 0)

            def pairs(b, start):
                for t in range(start, start + PAIRS // 2):
                    evac(b + 1, t)
                    if t + 3 < PAIRS:
                        exps(b, t + 3)
                    if t % 2 == 0:
                        save(b + 1, t // 2)

            first_half(0)
            with act.Fori(0, BLOCKS_A - 2) as b:
                pairs(b, PAIRS // 2)
                first_half(b + 1)
            pairs(BLOCKS_A - 2, PAIRS // 2)
            for t in range(PAIRS):
                exps(BLOCKS_A - 1, t)

            def factored(l):
                for s in (x_exp,) + ((x_eo,) if l == ELU_LAYER else ()):
                    act.sem_inc(s, BLOCKS_X)
                U, R = U_of[l], R_of[l]
                act.wait_ge(k_ready, l + 1)
                act.activation(B[:, :], U[:, :, D], ACT.Exp, bias=B_bias, scale=SLOPE).then_inc(bt_ready, 1)
                act.activation(T[:, :], U[:, :, D], ACT.Exp, bias=T_bias, scale=1.0 - SLOPE).then_inc(bt_ready, 1)

                def row_factor(q):
                    hold(act, rlin_ready, l * BLOCKS_G + q + 1)
                    act.activation(R[:, ds(q * WG, WG)], R[:, ds(q * WG, WG)], ACT.Exp,
                                   scale=-(1.0 - SLOPE)).then_inc(r_ready, 1)

                def exp_out(q):
                    act.wait_ge(neg_ready, q + 1)
                    act.activation(exp_o, neg_o, ACT.Exp).then_inc(expo_ready, 1)

                def block_g(last, more):
                    if last is not None:
                        if l == ELU_LAYER:
                            exp_out(last)
                        if l + 1 < LAYERS:
                            roots(l + 2, last, 0)
                            relu_T(l + 2, last, hT_blk)
                            projected(l + 1, last)
                    if more:
                        row_factor(last + 2 if last is not None else 1)

                row_factor(0)
                block_g(None, True)
                with act.Fori(0, BLOCKS_G - 2) as last:
                    block_g(last, True)
                block_g(BLOCKS_G - 2, False)
                block_g(BLOCKS_G - 1, False)

            def general(l):
                act.sem_inc(bt_ready, 2)
                act.sem_inc(r_ready, BLOCKS_G)
                if l == ELU_LAYER:
                    act.sem_inc(expo_ready, BLOCKS_G)
                with act.Fori(0, BLOCKS_X) as b:
                    act.wait_ge(x_sub, l * BLOCKS_X + b + 1)
                    act.activation(h_all, h_all, ACT.Exp).then_inc(x_exp, 1)
                    if l == ELU_LAYER:
                        act.wait_ge(x_neg, b + 1)
                        act.activation(exp_o[:, 0:D], neg_o[:, 0:D], ACT.Exp).then_inc(x_eo, 1)
                if l + 1 < LAYERS:
                    all_blocks(l + 2, spare_of[l + 1], l + 1)

            all_blocks(1, third[1], 0)
            for l in range(LAYERS):
                act.activation(warm, identF[:, 0:1], ACT.Exp)
                either_path(act, l, general, factored)

        @block.vector
        def _(dve):
            dve.sem_inc(p_made, CREDIT)
            dve.sem_inc(p_free, RING)
            dve.sem_inc(acc_free, 2)
            dve.sem_inc(x_masked, 1)
            dve.wait_ge(consts, CONSTS)

            dve.wait_ge(w_in_s, 16 * (4 + LAYERS))
            pro = Tally(dve_pro, 0)
            for l in range(LAYERS):
                pro.inc(dve.tensor_copy(WX[:, l, 0:D], Wraw[:, 1 + l, :]))
                pro.inc(dve.tensor_tensor_reduce(w_dot, Wraw[:, 1 + l, :], a_rows[:, l, 0:D], 1.0, 0.0, ALU.mult,
                                                 ALU.add, va1[:, l:l + 1]))
                pro.wait(dve)
                pro.inc(dve.tensor_tensor_reduce(w_dot, Wraw[:, 1 + l, :], a_rows[:, l, D:2 * D], 1.0, 0.0, ALU.mult,
                                                 ALU.add, WX[:, l, D:E]))
                pro.wait(dve)
            def split_keys(half):
                if half == 0:
                    dve.wait_ge(key_in, 16)
                    dve.tensor_copy(key_hi[:, :], third[2]).then_inc(key_split, 1)
                else:
                    dve.wait_ge(key_split, 1)
                    dve.tensor_tensor(key_lo[:, :], third[2], key_hi[:, :].bitcast(F32), ALU.subtract
                                      ).then_inc(key_split, 1)

            dve.memset(U0[:, :, D:E], 1.0).then_inc(wx_ready, 1)

            def moments(k, q, slot):
                n = turn(k, q)
                for c in range(SUB_G):
                    xs = X[:, ds(q * SUB_G + c, 1), :].rearrange("p o d -> p (o d)")
                    mm = dve.bn_stats(stats[:, c, :], xs)
                mm.then_inc(stat_ready, 1)
                hold(dve, stat_ready, n + 1)
                for c in range(SUB_G):
                    mm = dve.bn_aggr(mv[:, slot, c, :], stats[:, c, :])
                mm.then_inc(aggr_ready, 1)
                dve.wait_ge(aggr_ready, n + 1)
                dve.tensor_scalar(var[:, slot, :], mv[:, slot, :, 1], EPS, None, ALU.add).then_inc(var_ready, 1)

            def normalize(k, q, slot, h):
                n = k * BLOCKS_G + q
                dve.wait_ge(std_ready, n + 1)
                dve.reciprocal(rstd[:, slot, :], rstd[:, slot, :]).then_inc(rc_ready, 1)
                dve.wait_ge(rc_ready, n + 1)
                for c in range(SUB_G):
                    xs = X[:, ds(q * SUB_G + c, 1), :].rearrange("p o d -> p (o d)")
                    mm = dve.tensor_scalar(h[:, c * D:(c + 1) * D], xs, mv[:, slot, c, 0:1],
                                           rstd[:, slot, c:c + 1], ALU.subtract, ALU.mult)
                mm.then_inc(h_ready, 1)

            def low_g(q):
                for b in (2 * q + 1, 2 * q):
                    dve.wait_ge(g_half, BLOCKS_A - b)
                    dve.tensor_tensor(g_slot(b)[:, WA:2 * WA], bank(2 + b % 2, WA),
                                      g_slot(b)[:, 0:WA].bitcast(F32), ALU.subtract
                                      ).then_inc(g_made, 1)

            for i in range(BLOCKS_G + 4):
                q = BLOCKS_G - 1 - i
                if q >= 0:
                    if i % (BLOCKS_G // X_LOADS) == 0:
                        dve.wait_ge(x_in_s[i // (BLOCKS_G // X_LOADS)], 16)
                    if i >= SLOTS:
                        dve.wait_ge(h_ready, i - SLOTS + 1)
                    moments(0, q, i % SLOTS)
                if 0 <= q + 1 < BLOCKS_G:
                    slot = (i - 1) % SLOTS
                    dve.wait_ge(std_ready, i)
                    dve.reciprocal(rstd[:, slot, :], rstd[:, slot, :]).then_inc(rc_ready, 1)
                    dve.wait_ge(rc_ready, i)
                    dve.scalar_tensor_tensor(out=shift[:, slot, :], in0=mv[:, slot, :, 0], scalar=-1.0,
                                             in1=rstd[:, slot, :], op0=ALU.mult, op1=ALU.mult
                                             ).then_inc(shift_ready, 1)
                if 0 <= q + 4 < BLOCKS_G:
                    low_g(q + 4)
                if i == 4:
                    split_keys(0)
                if i == 9:
                    dve.wait_ge(g_staged, 16 * (BLOCKS_A - STAGED))
                    split_keys(1)

            def all_blocks(k):
                for q in range(BLOCKS_G + 1):
                    if k == 1 and q == LEAD + 1:
                        take(BLOCKS_A - 1)
                        dve.wait_ge(num_taken, BLOCKS_A)
                    if q < BLOCKS_G:
                        moments(k, q, q % 2)
                    if q >= 1:
                        if k == 1:
                            dve.wait_ge(av_done, (BLOCKS_A - 1) * PAIRS + q)
                        normalize(k, q - 1, (q - 1) % 2, h_all[:, (q - 1) * WG:q * WG])

            def no_edge(b, g):
                m = b * GROUPS + g
                dve.wait_ge(adj_in[g % 3], 16 * (b * (GROUPS // 3) + g // 3 + 1))
                if not isinstance(m, int) or m >= 3:
                    dve.wait_ge(scores_ready, 2 * (m - 2))
                    dve.wait_ge(save_made, m - 2)
                dve.tensor_scalar(notb[:, g % 3, :], adjb[:, g % 3, :], 0, None, ALU.is_le).then_inc(not_made, 1)

            def keep_max(b, t):
                n = b * PAIRS + t
                dve.wait_ge(scores_ready, n + 1)
                src = ps[:, 2 * (t % 3) * 512:(2 * (t % 3) + 2) * 512].rearrange("p (q w) -> p q w", q=2)[:, :, 0:WA]
                if t == 0:
                    dve.tensor_copy(run_max[:, :, :], src).then_inc(max_done, 1)
                else:
                    dve.wait_ge(max_done, n)
                    dve.tensor_tensor(run_max[:, :, :], run_max[:, :, :], src, ALU.max).then_inc(max_done, 1)

            def row_max(b):
                dve.wait_ge(max_done, (b + 1) * PAIRS)
                dve.tensor_tensor(part_max[:, :], run_max[:, 0, :], run_max[:, 1, :], ALU.max).then_inc(part_ready, 1)
                dve.wait_ge(mT_ready, b + 1)
                dve.tensor_reduce(max_c[:, :], bank(7, WA).rearrange("p (c w) -> p c w", w=P), AX.X,
                                  ALU.max).then_inc(mc_ready, 1)

            def sub(b, t):
                if t == 0:
                    dve.wait_ge(mb_ready, b + 1)
                dve.wait_ge(evac_done, b * PAIRS + t + 1)
                dve.tensor_tensor(S[:, 2 * t:2 * t + 2, :], S[:, 2 * t:2 * t + 2, :],
                                  bank(7, WA).unsqueeze(1).to_broadcast([P, 2, WA]), ALU.subtract
                                  ).then_inc(sub_done, 1)

            def take(b):
                dve.wait_ge(av_done, (b + 1) * PAIRS)
                acc = bank(6, SUB_A * E).rearrange("p (c k) -> p c k", k=E)
                dve.reciprocal(den_r[:, 0:SUB_A], acc[:, :, D]).then_inc(rden_ready, 1)
                dve.wait_ge(rden_ready, b + 1)
                for c in range(SUB_A):
                    xs = X[:, ds(b * SUB_A + c, 1), :].rearrange("p o d -> p (o d)")
                    mm = dve.scalar_tensor_tensor(out=xs, in0=acc[:, c, 0:D], scalar=den_r[:, c:c + 1], in1=xs,
                                                  op0=ALU.mult, op1=ALU.add)
                mm.then_inc(num_taken, 1)

            no_edge(0, 0)
            no_edge(0, 1)
            for t in range(PAIRS):
                keep_max(0, t)
                if t % 2 == 0 and t < PAIRS - 2:
                    g = t // 2 + 2
                    no_edge(g // GROUPS, g % GROUPS)
            row_max(0)
            sub(0, 0)
            no_edge(1, 1)

            def step_a(b):
                sub(b, 1)
                keep_max(b + 1, 0)
                sub(b, 2)
                keep_max(b + 1, 1)
                sub(b, 3)
                sub(b, 4)
                for t in range(PAIRS):
                    if t + 5 < PAIRS:
                        sub(b, t + 5)
                    if t % 2 == 0:
                        g = t // 2 + 2
                        if g < GROUPS:
                            no_edge(b + 1, g)
                        elif t < PAIRS - 2 and not (isinstance(b, int) and b == BLOCKS_A - 2):
                            no_edge(b + 2, g - GROUPS)
                    if t + 2 < PAIRS:
                        keep_max(b + 1, t + 2)
                row_max(b + 1)
                sub(b + 1, 0)
                take(b)
                if not (isinstance(b, int) and b == BLOCKS_A - 2):
                    no_edge(b + 2, 1)

            with dve.Fori(0, BLOCKS_A - 2) as b:
                step_a(b)
            step_a(BLOCKS_A - 2)
            for t in range(1, PAIRS):
                sub(BLOCKS_A - 1, t)

            PRE = 6

            def choose(l):
                U = U_of[l]
                own = Tally(pre_step, l * PRE)
                dve.wait_ge(wh_taken, 2 * (l + 1) * BLOCKS_G)
                own.inc(dve.tensor_reduce(dmin, U[:, :, D], AX.X, ALU.min))
                own.wait(dve)
                dve.tensor_reduce(dmax, U[:, :, D], AX.X, ALU.max).then_inc(dmm_ready, 1)
                dve.wait_ge(hT_ready, 2 * (l + 2) * BLOCKS_G)
                dve.tensor_reduce(hsum, hs_part[:, :], AX.X, ALU.add).then_inc(hsum_ready, 1)
                dve.wait_ge(dT_ready, l + 1)
                dve.tensor_reduce(k0s[0:1, :], ps[0:1, 6 * 512:6 * 512 + P], AX.X, ALU.max).then_inc(k0_ready, 1)
                own.inc(dve.tensor_reduce(k1s[0:1, :], ps[0:1, 6 * 512 + P:6 * 512 + 2 * P], AX.X, ALU.min))
                dve.wait_ge(k0_ready, l + 1)
                own.wait(dve)
                own.inc(dve.tensor_tensor(k1s[0:1, :], k0s[0:1, :], k1s[0:1, :], ALU.subtract))
                own.wait(dve)
                dve.tensor_scalar(path[:, :], k1s[0:1, :], SPREAD, None, ALU.is_gt).then_inc(path_ready, 1)
                dve.wait_ge(kb_ready, l + 1)
                own.inc(dve.tensor_copy(K0, bank(7, 1)))
                own.wait(dve)
                own.inc(dve.tensor_scalar(T_bias, K0, SLOPE - 1.0, None, ALU.mult))
                own.wait(dve)
                dve.tensor_scalar(B_bias, K0, -SLOPE, None, ALU.mult).then_inc(k_ready, 1)
                dve.wait_ge(sumb_ready, l + 1)
                own.inc(dve.tensor_copy(sum_b[:, :], bank(7, D)))
                dve.wait_ge(s_taken, 2 * (l + 1) * BLOCKS_G)
                own.wait(dve)
                assert own.n == PRE, own.n

            def factored(l):
                U, R = U_of[l], R_of[l]
                for s, n in ((x_ones, 2), (x_step, X_STEPS[l] * BLOCKS_X), (x_masked, BLOCKS_X),
                             (x_part, BLOCKS_X), (x_mc, BLOCKS_X), (x_sub, BLOCKS_X)):
                    dve.sem_inc(s, n)
                if l == ELU_LAYER:
                    dve.sem_inc(x_neg, BLOCKS_X)

                def row_factor(q):
                    rs = R[:, ds(q * WG, WG)]
                    dve.tensor_scalar(rs, rs, K0, 0.0, ALU.add, ALU.max).then_inc(rlin_ready, 1)

                def scale_values(c):
                    cs = slice(c * CHUNK, (c + 1) * CHUNK)
                    dve.tensor_tensor(U[:, cs, 0:D], U[:, cs, 0:D],
                                      B[:, cs].unsqueeze(2).to_broadcast([P, CHUNK, D]),
                                      ALU.mult).then_inc(u_ready, 1)
                    dve.tensor_copy(U[:, cs, D], B[:, cs]).then_inc(u_ready, 1)

                row_factor(0)
                dve.wait_ge(bt_ready, 2 * (l + 1))
                scale_values(0)

                def weights(q, j):
                    n = (l * BLOCKS_G + q) * TILES + j
                    s = j // SAVE
                    if j % SAVE == 0:
                        dve.wait_ge(mask_in[s % 2], 16 * ((l * BLOCKS_G + q) * 2 + s // 2 + 1))
                    hold(dve, p_free, n + 1)
                    two = "p (h w) -> p h w"
                    dve.scalar_tensor_tensor(out=pring[:, j % RING, :].rearrange(two, h=2),
                                             in0=R[:, ds(q * WG, WG)].rearrange(two, h=2), scalar=T[:, j:j + 1],
                                             in1=maskb[:, s % 2, :, j % SAVE, :], op0=ALU.max, op1=ALU.mult
                                             ).then_inc(p_made, 1)

                FIN = 6

                def finish1(q):
                    fin = Tally(fin_step, (l * BLOCKS_G + q) * FIN)
                    dve.wait_ge(p_free, (l * BLOCKS_G + q + 1) * TILES + RING)
                    empty, den, inv = (den_r[:, i * SUB_G:(i + 1) * SUB_G] for i in range(3))
                    accs = [ps[:, ds((q % 2) * 1024 + i * 512, 3 * E)].rearrange("p (c k) -> p c k", k=E)
                            for i in range(2)]
                    for i in range(2):
                        fin.inc(dve.tensor_scalar(empty[:, 3 * i:3 * i + 3], accs[i][:, :, D], 0.0, None,
                                                  ALU.is_equal))
                    fin.wait(dve)
                    for i in range(2):
                        fin.inc(dve.scalar_tensor_tensor(out=den[:, 3 * i:3 * i + 3], in0=empty[:, 3 * i:3 * i + 3],
                                                         scalar=float(N), in1=accs[i][:, :, D], op0=ALU.mult,
                                                         op1=ALU.add))
                    fin.wait(dve)
                    fin.inc(dve.reciprocal(inv, den))
                    for c in range(SUB_G):
                        mm = dve.scalar_tensor_tensor(out=o_buf[:, c * D:(c + 1) * D], in0=sum_b[:, :],
                                                      scalar=empty[:, c:c + 1], in1=accs[c // 3][:, c % 3, 0:D],
                                                      op0=ALU.mult, op1=ALU.add)
                    mm.then_inc(acc_free, 1)
                    dve.wait_ge(acc_free, l * BLOCKS_G + q + 1 + 2)
                    fin.wait(dve)
                    six = "p (c d) -> p c d"
                    fin.inc(dve.tensor_tensor(o_buf.rearrange(six, d=D), o_buf.rearrange(six, d=D),
                                              inv.unsqueeze(2).to_broadcast([P, SUB_G, D]), ALU.mult))
                    fin.wait(dve)
                    assert fin.n == FIN
                    if l == ELU_LAYER:
                        dve.tensor_scalar(neg_o, o_buf, 0.0, None, ALU.min).then_inc(neg_ready, 1)

                def finish2(q):
                    if l == ELU_LAYER:
                        dve.wait_ge(expo_ready, q + 1)
                        dve.tensor_scalar(exp_o, exp_o, -1.0, None, ALU.add).then_inc(elu_step, 1)
                        dve.wait_ge(elu_step, 2 * q + 1)
                        dve.scalar_tensor_tensor(out=o_buf, in0=o_buf, scalar=0.0, in1=exp_o, op0=ALU.max,
                                                 op1=ALU.add).then_inc(elu_step, 1)
                        dve.wait_ge(elu_step, 2 * q + 2)
                    xs = X[:, ds(q * SUB_G, SUB_G), :]
                    dve.tensor_tensor(xs, xs, o_buf.rearrange("p (c d) -> p c d", d=D), ALU.add).then_inc(x_done, 1)

                def block_g(q, last, more):
                    dve.wait_ge(r_ready, l * BLOCKS_G + q + 1)
                    for j in range(TILES):
                        if last is not None:
                            if j == 6:
                                finish1(last)
                            if j == 11:
                                finish2(last)
                            if l + 1 < LAYERS:
                                if j == 14:
                                    hold(dve, x_done, l * BLOCKS_G + last + 1)
                                    moments(l + 2, last, 0)
                                if j == 21:
                                    normalize(l + 2, last, 0, h_blk[:, :])
                        if j == 30 and more:
                            row_factor(q + 1)
                        if last is None and j % CHUNK == 4 and j // CHUNK + 1 < CHUNKS:
                            scale_values(j // CHUNK + 1)
                        weights(q, j)

                block_g(0, None, True)
                with dve.Fori(1, BLOCKS_G - 1) as q:
                    block_g(q, q - 1, True)
                block_g(BLOCKS_G - 1, BLOCKS_G - 2, False)
                finish1(BLOCKS_G - 1)
                finish2(BLOCKS_G - 1)
                if l + 1 < LAYERS:
                    dve.wait_ge(x_done, (l + 1) * BLOCKS_G)
                    moments(l + 2, BLOCKS_G - 1, 0)
                    normalize(l + 2, BLOCKS_G - 1, 0, h_blk[:, :])

            def general(l):
                U, R = U_of[l], R_of[l]
                M = spare_of[l]
                for s, n in ((rlin_ready, BLOCKS_G), (u_ready, 2 * CHUNKS), (p_made, BLOCKS_G * TILES),
                             (acc_free, BLOCKS_G), (fin_step, 6 * BLOCKS_G)):
                    dve.sem_inc(s, n)
                if l == ELU_LAYER:
                    dve.sem_inc(neg_ready, BLOCKS_G)
                    dve.sem_inc(elu_step, 2 * BLOCKS_G)
                dve.tensor_copy(B[:, :], U[:, :, D]).then_inc(x_ones, 1)
                dve.wait_ge(x_ones, 2 * l + 1)
                dve.memset(U[:, :, D:E], 1.0).then_inc(x_ones, 1)
                Sx = h_all.rearrange("p (t w) -> p t w", w=QUERIES)
                with dve.Fori(0, BLOCKS_X) as b:
                    n = l * BLOCKS_X + b
                    own = Tally(x_step, sum(X_STEPS[:l]) * BLOCKS_X + b * X_STEPS[l])
                    rows = R[:, ds(b * QUERIES, QUERIES)].unsqueeze(1).to_broadcast([P, TILES, QUERIES])
                    own.inc(dve.tensor_tensor(Sx, B[:, :].unsqueeze(2).to_broadcast([P, TILES, QUERIES]), rows,
                                              ALU.add))
                    own.wait(dve)
                    own.inc(dve.scalar_tensor_tensor(out=Sx, in0=Sx, scalar=SLOPE, in1=Sx, op0=ALU.mult, op1=ALU.max))
                    dve.wait_ge(x_mask_in, 16 * SAVES * (n + 1))
                    dve.tensor_scalar(M.rearrange("p (t w) -> p t w", w=QUERIES), maskx[:, :, :], -0.5, -2.0 * MASKED,
                                      ALU.add, ALU.mult).then_inc(x_masked, 1)
                    dve.wait_ge(x_masked, n + 2)
                    own.wait(dve)
                    own.inc(dve.tensor_tensor(h_all, h_all, M, ALU.min))
                    own.wait(dve)
                    dve.tensor_reduce(part_max[:, 0:P], Sx.rearrange("p t w -> p w t"), AX.X, ALU.max
                                      ).then_inc(x_part, 1)
                    dve.wait_ge(x_mT, n + 1)
                    dve.tensor_reduce(max_c[:, 0:1], bank(7, P), AX.X, ALU.max).then_inc(x_mc, 1)
                    dve.wait_ge(x_mb, n + 1)
                    dve.tensor_tensor(Sx, Sx, bank(7, P).unsqueeze(1).to_broadcast([P, TILES, QUERIES]),
                                      ALU.subtract).then_inc(x_sub, 1)
                    dve.wait_ge(x_av, n + 1)
                    own.inc(dve.reciprocal(den_r[:, 0:1], bank(6, E)[:, D:E]))
                    own.wait(dve)
                    own.inc(dve.tensor_scalar(o_buf[:, 0:D], bank(6, D), den_r[:, 0:1], None, ALU.mult))
                    own.wait(dve)
                    if l == ELU_LAYER:
                        dve.tensor_scalar(neg_o[:, 0:D], o_buf[:, 0:D], 0.0, None, ALU.min).then_inc(x_neg, 1)
                        dve.wait_ge(x_eo, b + 1)
                        own.inc(dve.tensor_scalar(exp_o[:, 0:D], exp_o[:, 0:D], -1.0, None, ALU.add))
                        own.wait(dve)
                        own.inc(dve.scalar_tensor_tensor(out=o_buf[:, 0:D], in0=o_buf[:, 0:D], scalar=0.0,
                                                         in1=exp_o[:, 0:D], op0=ALU.max, op1=ALU.add))
                        own.wait(dve)
                    xs = X[:, ds(b, 1), :].rearrange("p o d -> p (o d)")
                    own.inc(dve.tensor_tensor(xs, xs, o_buf[:, 0:D], ALU.add))
                    own.wait(dve)
                    assert own.n == X_STEPS[l], own.n
                dve.sem_inc(x_done, BLOCKS_G)
                if l + 1 < LAYERS:
                    all_blocks(l + 2)

            all_blocks(1)
            for l in range(LAYERS):
                choose(l)
                either_path(dve, l, general, factored)


def kernel(x, adj, L0_gnn_input, L0_gnn_weight, L1_gnn_W, L1_gnn_a, L2_gnn_W, L2_gnn_a, L3_gnn_W, L3_gnn_a):
    import numpy as np
    import concourse.bacc as bacc
    from concourse.bass_utils import run_bass_kernel_spmd

    def rows(a):
        return np.ascontiguousarray(np.asarray(a).reshape(TILES, P, D).transpose(1, 0, 2))

    adj_t = np.ascontiguousarray(
        np.asarray(adj).reshape(BLOCKS_A, WA, GROUPS, GROUP, P).transpose(0, 2, 4, 3, 1)
    ).reshape(BLOCKS_A, GROUPS, P, GROUP * WA)
    arrays = {
        "x": rows(x), "adj": adj_t, "values": rows(L0_gnn_input),
        "keys": np.ascontiguousarray(np.asarray(L0_gnn_input).T),
        "w0": np.asarray(L0_gnn_weight), "w1": np.asarray(L1_gnn_W), "w2": np.asarray(L2_gnn_W),
        "w3": np.asarray(L3_gnn_W),
        "a1": np.asarray(L1_gnn_a).reshape(1, 2 * D), "a2": np.asarray(L2_gnn_a).reshape(1, 2 * D),
        "a3": np.asarray(L3_gnn_a).reshape(1, 2 * D),
    }
    nc = bacc.Bacc("TRN2", target_bir_lowering=False, num_devices=1, dynamic_dma_scratch_size=256)
    t = {n: nc.dram_tensor(n + "_dram", a.shape, mybir.dt.from_np(a.dtype), kind="ExternalInput").ap()
         for n, a in arrays.items()}
    out = nc.dram_tensor("out_dram", (P, TILES, D), F32, kind="ExternalOutput").ap()
    mask_scr = nc.dram_tensor("mask_scr", (BLOCKS_A, SAVES, P, SAVE * WA), U8, kind="Internal").ap()
    g_scr = nc.dram_tensor("g_scr", (BLOCKS_A, P, 2 * WA), F32, kind="Internal").ap()
    program(nc, t["x"], t["adj"], t["values"], t["keys"], [t[f"w{i}"] for i in range(4)],
            [t[f"a{i}"] for i in range(1, 4)], mask_scr, g_scr, out)
    r = run_bass_kernel_spmd(nc, [{n + "_dram": a for n, a in arrays.items()}], core_ids=[0])
    return r.results[0]["out_dram"].transpose(1, 0, 2).reshape(N, D)
```
